# Optimizing a Trainium2 kernel written in Bass

```python
import numpy as np
import jax
import jax.numpy as jnp

def _softmax(x, axis=-1):
    return jax.nn.softmax(x, axis=axis)

def _gelu(x):
    return jax.nn.gelu(x, approximate=True)

def _silu(x):
    return jax.nn.silu(x)

def _sigmoid(x):
    return jax.nn.sigmoid(x)

def _layernorm(x, axis=-1, eps=1e-05):
    m = jnp.mean(x, axis=axis, keepdims=True)
    v = jnp.var(x, axis=axis, keepdims=True)
    return (x - m) / jnp.sqrt(v + eps)

def _scatter_add(tgt, idx, src, axis=0):
    return tgt.at[idx].add(src)

def _segment_sum(src, seg, n):
    return jax.ops.segment_sum(src, seg, n)
kernel_name = 'mk_metaformer_d1_conv_nchw128_r2_7d71d3'

def setup_inputs(seed: int=0):
    np.random.seed(seed)
    _w = jnp.asarray

    def _rec_inputs():
        import jax
        import jax.numpy as jnp
        _gk = jax.random.key(seed)
        x = 7.22e-05 + 1 * jax.random.normal(jax.random.fold_in(_gk, 1), (16, 64, 32, 32), jnp.float32)
        return x
    x = _rec_inputs()

    def _L0_conv_setup():
        import jax, jax.numpy as jnp
        import numpy as np
        from jax import lax

        def _conv2d_nchw(x, w, pad_h):
            return lax.conv_general_dilated(x, w, window_strides=(1, 1), padding=((pad_h, pad_h), (0, 0)), dimension_numbers=('NCHW', 'OIHW', 'NCHW'))
        key = jax.random.key(seed)
        ks = jax.random.split(key, 7)
        B, C, S, W = (16, 64, 32, 32)
        NH = 64
        return {'image': jax.random.normal(ks[0], (B, C, S, W), dtype=jnp.float32), 'w_itos': jax.random.normal(ks[1], (4 * NH, C, 3, 1), dtype=jnp.float32) * 0.05, 'b_itos': jax.random.normal(ks[2], (4 * NH,), dtype=jnp.float32) * 0.05, 'w_stos': jax.random.normal(ks[3], (4 * NH, NH, 3, 1), dtype=jnp.float32) * 0.05, 'b_stos': jax.random.normal(ks[4], (4 * NH,), dtype=jnp.float32) * 0.05, 'h0': jax.random.normal(ks[5], (NH, W, 1), dtype=jnp.float32), 'c0': jax.random.normal(ks[6], (NH, W, 1), dtype=jnp.float32)}
    _L0_conv_all = _L0_conv_setup()
    _L0_conv_in = {k: v for k, v in _L0_conv_all.items() if k in ('w_itos', 'b_itos', 'w_stos', 'b_stos', 'h0', 'c0')}
    del _L0_conv_all

    def _L0_ffn_setup():
        import jax, jax.numpy as jnp
        import numpy as np
        B, S, D, E, H, O, K = (256, 1024, 64, 32, 256, 64, 8)
        key = jax.random.key(seed)
        k0, k1, k2, k3 = jax.random.split(key, 4)
        x = jax.random.normal(k0, (B, S, D), dtype=jnp.float32)
        gate_w = jax.random.normal(k1, (E, D), dtype=jnp.float32) * (1.0 / np.sqrt(D))
        gate_b = jnp.zeros((E,), dtype=jnp.float32)
        weight1 = jax.random.uniform(k2, (E, D + 1, H), dtype=jnp.float32, minval=-1.0, maxval=1.0) * (1.0 / np.sqrt(D + 1))
        weight2 = jax.random.uniform(k3, (E, H + 1, O), dtype=jnp.float32, minval=-1.0, maxval=1.0) * (1.0 / np.sqrt(H + 1))
        return {'x': x, 'gate_w': gate_w, 'gate_b': gate_b, 'weight1': weight1, 'weight2': weight2}
    _L0_ffn_all = _L0_ffn_setup()
    _L0_ffn_in = {k: v for k, v in _L0_ffn_all.items() if k in ('gate_w', 'gate_b', 'weight1', 'weight2')}
    del _L0_ffn_all
    return {'x': x, 'L0_conv_w_itos': _L0_conv_in['w_itos'], 'L0_conv_b_itos': _L0_conv_in['b_itos'], 'L0_conv_w_stos': _L0_conv_in['w_stos'], 'L0_conv_b_stos': _L0_conv_in['b_stos'], 'L0_conv_h0': _L0_conv_in['h0'], 'L0_conv_c0': _L0_conv_in['c0'], 'L0_ffn_gate_w': _L0_ffn_in['gate_w'], 'L0_ffn_gate_b': _L0_ffn_in['gate_b'], 'L0_ffn_weight1': _L0_ffn_in['weight1'], 'L0_ffn_weight2': _L0_ffn_in['weight2']}

def reference(x, L0_conv_w_itos, L0_conv_b_itos, L0_conv_w_stos, L0_conv_b_stos, L0_conv_h0, L0_conv_c0, L0_ffn_gate_w, L0_ffn_gate_b, L0_ffn_weight1, L0_ffn_weight2):
    import jax
    import jax.numpy as jnp

    def _L0_conv_ref(image, w_itos, b_itos, w_stos, b_stos, h0, c0):
        import jax, jax.numpy as jnp
        import numpy as np
        from jax import lax

        def _conv2d_nchw(x, w, pad_h):
            return lax.conv_general_dilated(x, w, window_strides=(1, 1), padding=((pad_h, pad_h), (0, 0)), dimension_numbers=('NCHW', 'OIHW', 'NCHW'))
        B = image.shape[0]
        mask = jnp.ones_like(w_itos).at[:, :, 2:, :].set(0.0)
        fs = _conv2d_nchw(image, w_itos * mask, pad_h=1) + b_itos[None, :, None, None]
        fs_t = jnp.moveaxis(fs, 2, 0)
        h = jnp.broadcast_to(h0[None], (B,) + h0.shape)
        c = jnp.broadcast_to(c0[None], (B,) + c0.shape)

        def step(carry, f_j):
            h, c = carry
            pre = _conv2d_nchw(h, w_stos, pad_h=1) + b_stos[None, :, None, None] + f_j[..., None]
            i, g, f, o = jnp.split(pre, 4, axis=1)
            c_new = jax.nn.sigmoid(f) * c + jax.nn.sigmoid(i) * jnp.tanh(g)
            h_new = c * jax.nn.sigmoid(o)
            return ((h_new, c_new), h_new)
        _, hs = lax.scan(step, (h, c), fs_t)
        return jnp.moveaxis(hs[..., 0], 0, 2)

    def _L0_ffn_ref(x, gate_w, gate_b, weight1, weight2):
        import jax, jax.numpy as jnp
        import numpy as np
        B, S, D, E, H, O, K = (256, 1024, 64, 32, 256, 64, 8)
        Bn, Sn, Dn = x.shape
        logits = jnp.einsum('bsd,ed->bse', x, gate_w) + gate_b
        probs = jax.nn.softmax(logits, axis=1)
        vals, idx = jax.lax.top_k(probs.transpose(0, 2, 1), K)
        topv = vals.transpose(0, 2, 1)
        topi = idx.transpose(0, 2, 1)
        flat_idx = topi.reshape(Bn, K * E)
        gathered = jnp.take_along_axis(x, flat_idx[:, :, None], axis=1)
        gathered = gathered.reshape(Bn, K, E, Dn)
        pooled = jnp.einsum('bked,bke->bed', gathered, topv)
        ones = jnp.ones((E, Bn, 1), dtype=x.dtype)
        h = jnp.concatenate([pooled.transpose(1, 0, 2), ones], axis=-1)
        h = jax.nn.gelu(jnp.einsum('ebd,edh->ebh', h, weight1), approximate=False)
        h = jnp.concatenate([h, ones], axis=-1)
        out = jnp.einsum('ebh,eho->ebo', h, weight2)
        out = out.transpose(1, 0, 2)
        weighted = jnp.einsum('beo,bke->bkeo', out, topv).reshape(Bn, K * E, O)
        outputs = jnp.zeros((Bn, Sn, O), dtype=x.dtype)
        outputs = outputs.at[jnp.arange(Bn)[:, None], flat_idx].add(weighted)
        return outputs

    def _gn(v, G=32, eps=1e-05):
        B_, C_, H_, W_ = v.shape
        g = v.reshape(B_, G, C_ // G, H_, W_)
        m = jnp.mean(g, axis=(2, 3, 4), keepdims=True)
        s = jnp.var(g, axis=(2, 3, 4), keepdims=True)
        return ((g - m) / jnp.sqrt(s + eps)).reshape(v.shape)

    def _ln_c(v, eps=1e-06):
        m = jnp.mean(v, axis=1, keepdims=True)
        s = jnp.var(v, axis=1, keepdims=True)
        return (v - m) / jnp.sqrt(s + eps)

    def _ln_t(v, eps=1e-05):
        m = jnp.mean(v, axis=-1, keepdims=True)
        s = jnp.var(v, axis=-1, keepdims=True)
        return (v - m) / jnp.sqrt(s + eps)

    def _to_tokens(v):
        B_, C_, H_, W_ = v.shape
        return v.reshape(B_, C_, H_ * W_).transpose(0, 2, 1)

    def _from_tokens(t, like):
        B_, C_, H_, W_ = like.shape
        return t.transpose(0, 2, 1).reshape(B_, C_, H_, W_)
    x = x + _L0_conv_ref(_ln_c(x), L0_conv_w_itos, L0_conv_b_itos, L0_conv_w_stos, L0_conv_b_stos, L0_conv_h0, L0_conv_c0)
    t = _to_tokens(x)
    t = t + _L0_ffn_ref(_ln_t(t), L0_ffn_gate_w, L0_ffn_gate_b, L0_ffn_weight1, L0_ffn_weight2)
    x = _from_tokens(t, x)
    return x

_drawn_inputs = setup_inputs


def setup_inputs(seed=0):
    import zlib

    import numpy as np

    out = dict(_drawn_inputs(seed))
    spreads = {'L0_ffn_gate_b': (0.0, 0.1)}
    factors = {'L0_conv_b_stos': 3.137,
     'L0_ffn_gate_w': 8.0,
     'L0_ffn_weight1': 8.0,
     'L0_ffn_weight2': 8.0}
    for name, (base, spread) in spreads.items():
        noise = np.random.default_rng([zlib.crc32(name.encode()), seed]).standard_normal(out[name].shape)
        drawn = base * np.exp(spread * noise) if base else spread * noise
        out[name] = jnp.asarray(drawn.astype(out[name].dtype))
    for name, factor in factors.items():
        out[name] = (out[name] * factor).astype(out[name].dtype)
    return out
```

```python
from contextlib import ExitStack

import concourse.bass as bass
from concourse import mybir

F32 = mybir.dt.float32
F16 = mybir.dt.float16
ACT = mybir.ActivationFunctionType
ALU = mybir.AluOpType
AX = mybir.AxisListType

B, C, S, W = 16, 64, 32, 32
E, K, H = 32, 8, 256
NB = B // 2
COLS = NB * W
RT = 4
TOK = RT * W
NT = S // RT
NG = NB // 2
QUAD = 4
GATES = 4 * C
GATE_ORDER = (3, 2, 0, 1)
PAD = W + 2
EPS_CONV, EPS_FFN = 1e-6, 1e-5
DMA = 16
BN = 6


class Tile:

    def __init__(self, n, half, par):
        self.n, self.half, self.par = n, half, par

    def shift(self, d):
        p = self.par + d
        return Tile(self.n + d, self.half + p // 2, p % 2)


def known(v):
    return isinstance(v, int)


def wait(eng, sem, value):
    if not known(value) or value > 0:
        eng.wait_ge(sem, value)


def metaformer(nc, x, w_itos, b_itos, w_stos, b_stos, h0, c0, gate_w, gate_b, w1, w2, out, scratch0, scratch1):
    ctx = ExitStack()
    with ctx:
        def sb(name, shape, dt=F32):
            return ctx.enter_context(nc.sbuf_tensor(name, shape, dt))

        def sem(name):
            return ctx.enter_context(nc.semaphore(name))

        ident = sb("ident", [128, 128])
        w_rows = sb("w_rows", [128, 2, 2, 3 * C])
        w_mean = sb("w_mean", [128, 2, 2])
        w_stack = sb("w_stack", [128, 2, 5, 128])
        w_hi = sb("w_hi", [128, 5, GATES], F16)
        w_lo = sb("w_lo", [128, 5, GATES], F16)
        b_rows = sb("b_rows", [4, 2, 2 * C])
        bias = sb("bias", [128, 4])
        gw_rows = sb("gw_rows", [2 * E, 2 * C])
        gw_mean = sb("gw_mean", [2 * E, 1])
        gw = sb("gw", [128, 2 * E])
        gbias = sb("gbias", [128, 1])
        pow_exp = sb("pow_exp", [128, B])
        w1s = sb("w1s", [C + 1, E, H])
        w2s = sb("w2s", [128, 2, E, C])
        b2_rows = sb("b2_rows", [E, C])
        b2 = sb("b2", [C, E])
        xin = sb("xin", [128, 2, NB, TOK])
        xres = sb("xres", [128, 2, NB, TOK])
        st0 = sb("st0", [128, B, BN])
        v0 = sb("v0", [128, 4, B])
        r0 = sb("r0", [128, B])
        r0t = sb("r0t", [B, TOK])
        rb_xr = sb("rb_xr", [128, 2, NB * TOK])
        rb = rb_xr[:, 0, :].rearrange("p (b t) -> p b t", b=NB)
        xr = rb_xr[:, 1, :].rearrange("p (s b w) -> p s b w", s=RT, b=NB)
        x_hi = sb("x_hi", [128, RT, COLS], F16)
        x_lo = sb("x_lo", [128, RT, COLS], F16)
        x_stk = [[sb(f"x_stk{p}{h}", [128, RT, COLS], F16) for h in range(2)] for p in range(2)]
        h_stk = [[sb(f"h_stk{p}{h}", [128, NB, PAD], F16) for h in range(2)] for p in range(2)]
        sg_o = sb("sg_o", [128, COLS])
        sg_f = sb("sg_f", [128, COLS])
        sg_i = sb("sg_i", [128, COLS])
        th_g = sb("th_g", [128, COLS])
        h32 = sb("h32", [128, 2, COLS])
        cell = sb("cell", [128, 2, COLS])
        fc = sb("fc", [128, COLS])
        ig = sb("ig", [128, COLS])
        x1t = sb("x1t", [128, 2, NB, TOK])
        x1f = sb("x1f", [128, NB, NT, TOK])
        xtok = sb("xtok", [128, NT, B, C])
        st1 = sb("st1", [128, B, BN])
        v1 = sb("v1", [128, 4, B])
        r1 = sb("r1", [128, B])
        r1t = sb("r1t", [B, TOK])
        rfs = sb("rfs", [128, NT, B])
        rbf = sb("rbf", [128, NG, TOK])
        lgr = sb("lgr", [128, NG, TOK])
        lg = sb("lg", [128, NG, NT, TOK])
        top = sb("top", [128, NG, K])
        top_e = sb("top_e", [128, NG, K])
        gb_max = sb("gb_max", [128, NG])
        gb_sub = sb("gb_sub", [128, NG])
        esum = sb("esum", [128, NG])
        rsum = sb("rsum", [128, NG])
        pooled = sg_o[:, :].rearrange("p (g c) -> p g c", c=C)
        pmean = sb("pmean", [128, NG])
        mask = sb("mask", [128, 2])
        rmask = sb("rmask", [128, NG, 2])
        unpicked = [xin[:, p, :, :].rearrange("p b t -> p (b t)") for p in range(2)]
        hid = xres[:, :, :, :].rearrange("p a b t -> p (a b t)").rearrange("p (q h) -> p q h", h=H)
        hid_t = rb_xr[:, :, :].rearrange("p a (q k j) -> p (a q) k j", k=2, j=128)
        pool_t = w_stack[0:C + 1, :, :, :].rearrange("p a n k -> p (a n k)")[:, 0:2 * B * E] \
            .rearrange("p (e i) -> p e i", e=E)
        o_t = h32[0:C, :, :].rearrange("p a (i e) -> p (a i) e", e=E)
        o_blk = cell[:, :, :].rearrange("p a (g h c) -> p (a g) h c", h=2, c=C)
        pick_t = x1t[:, :, :, :]
        y = xin[:, :, :, :].rearrange("p a b t -> p a (b t)")

        psum = [ctx.enter_context(nc.psum_tensor(f"ps{i}", [128, 512], F32)) for i in range(8)]
        ps_of, ps_ig = psum[0:2], psum[2:4]
        ps_t = psum[4:6]
        ps_lg, ps_r = psum[6], psum[7]
        PICK_BANKS = psum[4:6] + psum[0:2]
        HID_BANKS = psum[0:2] + psum[4:6]
        HT_BANKS = psum[2:4] + psum[6:8]
        Y_BANKS = psum[4:8]

        s_const = sem("s_const")
        s_const2 = sem("s_const2")
        s_wld = sem("s_wld")
        s_wld2 = sem("s_wld2")
        s_mask = sem("s_mask")
        s_wbias = sem("s_wbias")
        s_gws = sem("s_gws")
        s_gwt = sem("s_gwt")
        s_gwc = sem("s_gwc")
        s_lgr = sem("s_lgr")
        s_rsum = sem("s_rsum")
        s_wstep = sem("s_wstep")
        s_wt = sem("s_wt")
        s_whi = sem("s_whi")
        s_wlo = sem("s_wlo")
        s_w12 = sem("s_w12")
        s_zero = sem("s_zero")
        s_init = sem("s_init")
        s_xin = [sem(f"s_xin{p}") for p in range(2)]
        s_xres = [sem(f"s_xres{p}") for p in range(2)]
        s_p0t = sem("s_p0t")
        s_bn0 = sem("s_bn0")
        s_fin0 = sem("s_fin0")
        s_r0 = sem("s_r0")
        s_r0t = sem("s_r0t")
        s_r0c = sem("s_r0c")
        s_scr0 = sem("s_scr0")
        s_rb = sem("s_rb")
        s_xr = sem("s_xr")
        s_xhi = sem("s_xhi")
        s_xlo = sem("s_xlo")
        s_stk = sem("s_stk")
        s_conv = sem("s_conv")
        s_gof = sem("s_gof")
        s_gig = sem("s_gig")
        s_so = sem("s_so")
        s_sf = sem("s_sf")
        s_ig = sem("s_ig")
        s_h32 = sem("s_h32")
        s_hhi = sem("s_hhi")
        s_hlo = sem("s_hlo")
        s_cell = sem("s_cell")
        s_prod = sem("s_prod")
        s_x1 = sem("s_x1")
        s_x1f = sem("s_x1f")
        s_ft = sem("s_ft")
        s_xtok = sem("s_xtok")
        s_bn1 = sem("s_bn1")
        s_fin1 = sem("s_fin1")
        s_r1 = sem("s_r1")
        s_rfs = sem("s_rfs")
        s_r1t = sem("s_r1t")
        s_r1c = sem("s_r1c")
        s_scr1 = sem("s_scr1")
        s_rbf = sem("s_rbf")
        s_lg = sem("s_lg")
        s_lgm = sem("s_lgm")
        s_top = sem("s_top")
        s_sub = sem("s_sub")
        s_exp = sem("s_exp")
        s_tope = sem("s_tope")
        s_unp = sem("s_unp")
        s_pick = sem("s_pick")
        s_pt = sem("s_pt")
        s_ptm = sem("s_ptm")
        s_pool = sem("s_pool")
        s_pe = sem("s_pe")
        s_po = sem("s_po")
        s_pot = sem("s_pot")
        s_hid = sem("s_hid")
        s_gelu = sem("s_gelu")
        s_ht = sem("s_ht")
        s_hte = sem("s_hte")
        s_o = sem("s_o")
        s_oe = sem("s_oe")
        s_ot = sem("s_ot")
        s_ob = sem("s_ob")
        s_y = sem("s_y")
        s_ye = sem("s_ye")
        s_out = [sem(f"s_out{p}") for p in range(2)]

        x_cm = x.rearrange("(a b) c s w -> a c b (s w)", a=2)
        out_cm = out.rearrange("(a b) c s w -> a c b (s w)", a=2)

        NSTK = 4

        def half(h):
            return slice(C * h, C * h + C)

        def hi_rows(h):
            return slice(C * h, C * h + C)

        def lo_rows(h):
            return slice(C * (1 - h), C * (1 - h) + C)

        block = ctx.enter_context(nc.Block())

        @block.sync
        def _(q):
            def load_xin(t):
                if not (known(t.n) and t.n < 2):
                    q.wait_ge(s_xr, t.n - 1)
                for h in range(2):
                    q.dma_start(xin[half(h), t.par, :, :], x_cm[h, :, :, bass.ds(t.n * TOK, TOK)]) \
                        .then_inc(s_xin[t.par], DMA)

            def load_xres(t):
                if not (known(t.n) and t.n < 2):
                    q.wait_ge(s_x1, RT * (t.n - 1))
                for h in range(2):
                    q.dma_start(xres[half(h), t.par, :, :], x_cm[h, :, :, bass.ds(t.n * TOK, TOK)]) \
                        .then_inc(s_xres[t.par], DMA)

            def spread_r0(t):
                q.wait_ge(s_r0c, t.n + 1)
                q.dma_start(scratch0[:, :], r0t[:, :]).then_inc(s_scr0, DMA)
                q.wait_ge(s_scr0, DMA * (t.n + 1))
                wait(q, s_xr, t.n)
                for h in range(2):
                    q.dma_start(rb[half(h), :, :],
                                scratch0.rearrange("(b h) t -> h b t", h=2)[h].partition_broadcast(C)) \
                        .then_inc(s_rb, DMA)

            def stack_x(t):
                q.wait_ge(s_xlo, t.n + 1)
                if not (known(t.n) and t.n < 1):
                    q.wait_ge(s_conv, RT * t.n - 3)
                for h in range(2):
                    stk = x_stk[t.par][h]
                    q.dma_start(stk[0:C, :, :], x_hi[half(h), :, :]).then_inc(s_stk, DMA)
                    q.dma_start(stk[C:2 * C, :, :], x_lo[half(h), :, :]).then_inc(s_stk, DMA)

            def spread_r1(t):
                q.wait_ge(s_r1c, t.n + 1)
                q.dma_start(scratch1[:, :], r1t[:, :]).then_inc(s_scr1, DMA)
                q.wait_ge(s_scr1, DMA * (t.n + 1))
                wait(q, s_lgm, t.n)
                r_g = scratch1.rearrange("(g q) t -> q g t", q=QUAD)
                for k in range(QUAD):
                    q.dma_start(rbf[E * k:E * k + E, :, :], r_g[k].partition_broadcast(E)).then_inc(s_rbf, DMA)

            def keep_x1(t):
                q.wait_ge(s_x1, RT * (t.n + 1))
                q.dma_start(x1f[:, :, bass.ds(t.n, 1), :], x1t[:, t.par, :, :].unsqueeze(2)).then_inc(s_x1f, DMA)

            def phase(t, first=False, last=False):
                if not last:
                    if not first:
                        load_xin(t.shift(1))
                    load_xres(t.shift(1))
                if not first:
                    keep_x1(t.shift(-1))
                if not last:
                    spread_r0(t.shift(1))
                    stack_x(t.shift(1))
                if not first:
                    spread_r1(t.shift(-1))

            t0, t7 = Tile(0, 0, 0), Tile(NT - 1, (NT - 1) // 2, 1)
            load_xin(t0)
            for a in range(2):
                for n, w in enumerate((w_itos, w_stos)):
                    q.dma_start(w_rows[:, a, n, :], w[128 * a:128 * a + 128].rearrange("o c k one -> o (c k one)")) \
                        .then_inc(s_wld, DMA)
            load_xin(t0.shift(1))
            for h in range(2):
                q.dma_start(h32[half(h), 1, :].rearrange("p (b w) -> p b w", w=W),
                            h0.rearrange("c w one -> c one w").to_broadcast([C, NB, W])).then_inc(s_init, DMA)
                q.dma_start(cell[half(h), 0, :].rearrange("p (b w) -> p b w", w=W),
                            c0.rearrange("c w one -> c one w").to_broadcast([C, NB, W])).then_inc(s_init, DMA)
            for h in range(2):
                for n, b in enumerate((b_itos, b_stos)):
                    q.dma_start(b_rows[:, n, half(h)], b.rearrange("(g c) -> g c", c=C)).then_inc(s_wld2, DMA)
            q.wait_ge(s_zero, 1)
            for h in range(2):
                q.dma_start(gw_rows[E * h:E * h + E, C * h:C * h + C], gate_w).then_inc(s_wld2, DMA)
            for k in range(QUAD):
                q.dma_start(gbias[E * k:E * k + E, :], gate_b.unsqueeze(1)).then_inc(s_wld2, DMA)
            load_xres(t0)
            q.dma_start(b2_rows[:, :], w2[:, H, :]).then_inc(s_wld2, DMA)
            spread_r0(t0)
            stack_x(t0)
            phase(t0, first=True)
            q.dma_start(w1s[:, :, :], w1.rearrange("e k h -> k e h")).then_inc(s_w12, DMA)
            for k in range(2):
                q.dma_start(w2s[:, k, :, :], w2[:, 128 * k:128 * k + 128, :].rearrange("e k o -> k e o")) \
                    .then_inc(s_w12, DMA)
            with q.Fori(0, (NT - 2) // 2) as k:
                t = Tile(2 * k + 1, k, 1)
                phase(t)
                phase(t.shift(1))
            phase(t7, last=True)
            keep_x1(t7)
            spread_r1(t7)
            for b in range(NB):
                q.wait_ge(s_ye, 2 * b + 2)
                for h in range(2):
                    q.dma_start(out_cm[h, :, b, :], y[half(h), b % 2, :]).then_inc(s_out[b % 2], DMA)
            for p in range(2):
                q.wait_ge(s_out[p], DMA * NB)

        @block.gpsimd
        def _(p):
            p.memset(gw_rows[:, :], 0.0).then_inc(s_zero, 1)
            p.memset(ident[:, :], 0.0).then_inc(s_const, 1)
            p.wait_ge(s_const, 1)
            p.affine_select(out=ident[:, :], in_=ident[:, :], compare_op=ALU.not_equal, fill=1.0,
                            base=0, pattern=[[-1, 128]], channel_multiplier=1).then_inc(s_const, 1)
            p.memset(pow_exp[:, :], -0.5).then_inc(s_const, 1)
            for par in range(2):
                for h in range(2):
                    p.memset(h_stk[par][h][:, :, :], 0.0).then_inc(s_const, 1)
            for h in range(2):
                p.memset(x_stk[1][h][:, RT - 1, :], 0.0).then_inc(s_const, 1)

            def rsqrt0(t):
                p.wait_ge(s_fin0, 5 * (t.n + 1))
                wait(p, s_r0t, t.n)
                p.tensor_tensor(r0[:, :], v0[:, 1, :], pow_exp[:, :], ALU.pow).then_inc(s_r0, 1)

            def rsqrt1(t):
                p.wait_ge(s_fin1, 5 * (t.n + 1))
                wait(p, s_r1t, t.n)
                wait(p, s_rfs, t.n)
                p.tensor_tensor(r1[:, :], v1[:, 1, :], pow_exp[:, :], ALU.pow).then_inc(s_r1, 1)

            def residual(t, i):
                n = RT * t.n + i
                if i == 0:
                    p.wait_ge(s_xres[t.par], 2 * DMA * (t.half + 1))
                    if not (known(t.n) and t.n < 2):
                        p.wait_ge(s_x1f, DMA * (t.n - 1))
                        p.wait_ge(s_lg, t.n - 1)
                p.wait_ge(s_h32, n + 1)
                rows = slice(W * i, W * i + W)
                p.tensor_tensor(x1t[:, t.par, :, rows], xres[:, t.par, :, rows],
                                h32[:, i % 2, :].rearrange("p (b w) -> p b w", w=W), ALU.add).then_inc(s_x1, 1)

            def scale_logits(t):
                p.wait_ge(s_lgr, t.n + 1)
                p.wait_ge(s_rbf, QUAD * DMA * (t.n + 1))
                p.tensor_tensor(lg[:, :, bass.ds(t.n, 1), :], lgr[:, :, :].unsqueeze(2), rbf[:, :, :].unsqueeze(2),
                                ALU.mult).then_inc(s_lgm, 1)

            def phase(t, first=False, last=False):
                residual(t, 0)
                if not last:
                    rsqrt0(t.shift(1))
                residual(t, 1)
                residual(t, 2)
                if not first:
                    rsqrt1(t.shift(-1))
                residual(t, 3)
                if not first:
                    scale_logits(t.shift(-1))

            t0, t7 = Tile(0, 0, 0), Tile(NT - 1, (NT - 1) // 2, 1)
            rsqrt0(t0)
            p.wait_ge(s_wt, 5)
            p.memset(pool_t[:, :, :], 0.0).then_inc(s_const2, 1)
            p.wait_ge(s_const2, 1)
            p.memset(pool_t[C:C + 1, :, :], 1.0).then_inc(s_const2, 1)
            p.wait_ge(s_const2, 2)
            phase(t0, first=True)
            with p.Fori(0, (NT - 2) // 2) as k:
                t = Tile(2 * k + 1, k, 1)
                phase(t)
                phase(t.shift(1))
            phase(t7, last=True)
            rsqrt1(t7)
            scale_logits(t7)

        @block.scalar
        def _(a):
            def row_scale_parts(t):
                a.wait_ge(s_xr, t.n + 1)
                wait(a, s_stk, DMA * NSTK * t.n)
                a.activation(x_hi[:, :, :], xr[:, :, :, :].rearrange("p s b w -> p s (b w)"), ACT.Copy) \
                    .then_inc(s_xhi, 1)

            def hi_part(n, slot, par):
                for h in range(2):
                    a.activation(h_stk[par][h][hi_rows(h), :, 1:W + 1],
                                 h32[half(h), slot, :].rearrange("p (b w) -> p b w", w=W), ACT.Copy) \
                        .then_inc(s_hhi, 1)

            def step(t, i):
                n, par = RT * t.n + i, i % 2
                a.wait_ge(s_gof, n + 1)
                wait(a, s_h32, n)
                a.activation(sg_o[:, :], ps_of[par][:, 0:COLS], ACT.Sigmoid, bias=bias[:, 3:4]).then_inc(s_so, 1)
                wait(a, s_cell, n)
                a.activation(sg_f[:, :], ps_of[par][:, COLS:2 * COLS], ACT.Sigmoid, bias=bias[:, 2:3]) \
                    .then_inc(s_sf, 1)
                a.wait_ge(s_h32, n + 1)
                hi_part(n, par, 1 - par)
                a.wait_ge(s_gig, n + 1)
                a.activation(sg_i[:, :], ps_ig[par][:, 0:COLS], ACT.Sigmoid, bias=bias[:, 0:1]).then_inc(s_ig, 1)
                a.activation(th_g[:, :], ps_ig[par][:, COLS:2 * COLS], ACT.Tanh, bias=bias[:, 1:2]) \
                    .then_inc(s_ig, 1)

            def keep_tokens(t):
                for k in range(2):
                    a.wait_ge(s_ft, 2 * t.n + k + 1)
                    a.activation(xtok[:, bass.ds(t.n, 1), 8 * k:8 * k + 8, :].rearrange("p t b c -> p t (b c)"),
                                 ps_t[k][:, :].unsqueeze(1), ACT.Copy).then_inc(s_xtok, 1)

            def keep_logits(t):
                a.wait_ge(s_lg, t.n + 1)
                wait(a, s_lgm, t.n)
                a.activation(lgr[:, :, :].rearrange("p g t -> p (g t)"), ps_lg[:, :], ACT.Copy).then_inc(s_lgr, 1)

            def phase(t, first=False, last=False):
                step(t, 0)
                step(t, 1)
                if not first:
                    keep_tokens(t.shift(-1))
                step(t, 2)
                if not first:
                    keep_logits(t.shift(-1))
                if not last:
                    row_scale_parts(t.shift(1))
                step(t, 3)

            for n in range(5):
                a.wait_ge(s_wt, min(n // 2 * 2 + 2, 5))
                a.activation(w_hi[:, n, :], psum[4 + n // 2][:, GATES * (n % 2):GATES * (n % 2) + GATES], ACT.Copy) \
                    .then_inc(s_whi, 1)
            a.wait_ge(s_init, 4 * DMA)
            a.wait_ge(s_const, 7)
            hi_part(-1, 1, 0)
            t0, t7 = Tile(0, 0, 0), Tile(NT - 1, (NT - 1) // 2, 1)
            row_scale_parts(t0)
            a.wait_ge(s_wbias, 1)
            phase(t0, first=True)
            with a.Fori(0, (NT - 2) // 2) as k:
                t = Tile(2 * k + 1, k, 1)
                phase(t)
                phase(t.shift(1))
            phase(t7, last=True)
            keep_tokens(t7)
            keep_logits(t7)

            for g in range(NG):
                a.wait_ge(s_sub, 2 * g + 2)
                tokens = lg[:, g, :, :].rearrange("p t k -> p (t k)")
                a.activation(tokens, tokens, ACT.Exp, bias=gb_sub[:, g:g + 1], accum_out=esum[:, g:g + 1]) \
                    .then_inc(s_exp, 1)
                a.activation(top_e[:, g, :], top[:, g, :], ACT.Exp, bias=gb_sub[:, g:g + 1]).then_inc(s_exp, 1)
            a.wait_ge(s_po, 1)
            a.wait_ge(s_const2, 2)
            a.activation(pool_t[0:C, :, 0:B], psum[3][0:C, :].rearrange("p (i e) -> p e i", e=E), ACT.Copy) \
                .then_inc(s_pot, 1)
            for k in range(4):
                a.wait_ge(s_hid, k + 1)
                a.activation(hid[:, 2 * k:2 * k + 2, :].rearrange("p q h -> p (q h)"), HID_BANKS[k][:, :], ACT.Gelu) \
                    .then_inc(s_gelu, 1)

        @block.vector
        def _(v):
            def variances(t, st, var, s_bn, count, s_fin, s_r, eps):
                v.wait_ge(s_bn, count)
                wait(v, s_r, t.n)
                v.tensor_tensor(var[:, 0, :], st[:, :, 1], st[:, :, 4], ALU.subtract).then_inc(s_fin, 1)
                v.tensor_scalar(var[:, 1, :], st[:, :, 2], 1.0 / C, eps, ALU.mult, ALU.add).then_inc(s_fin, 1)
                v.wait_ge(s_fin, 5 * t.n + 2)
                v.scalar_tensor_tensor(var[:, 2, :], var[:, 0, :], 0.25, var[:, 0, :], ALU.mult, ALU.mult) \
                    .then_inc(s_fin, 1)
                v.scalar_tensor_tensor(var[:, 3, :], st[:, :, 5], 1.0 / C, var[:, 1, :], ALU.mult, ALU.add) \
                    .then_inc(s_fin, 1)
                v.wait_ge(s_fin, 5 * t.n + 4)
                v.tensor_tensor(var[:, 1, :], var[:, 2, :], var[:, 3, :], ALU.add).then_inc(s_fin, 1)

            def stats0(t):
                wait(v, s_fin0, 5 * t.n)
                for k in range(2):
                    v.wait_ge(s_p0t, 2 * t.n + k + 1)
                    for b in range(8):
                        ins = v.bn_stats(st0[:, 8 * k + b, :], ps_t[k][:, C * b:C * b + C])
                    ins.then_inc(s_bn0, 1)
                variances(t, st0, v0, s_bn0, 2 * t.n + 2, s_fin0, s_r0, EPS_CONV)

            def keep_r0t(t):
                v.wait_ge(s_r0t, t.n + 1)
                wait(v, s_scr0, DMA * t.n)
                v.tensor_copy(r0t[:, :], ps_r[0:B, 0:TOK]).then_inc(s_r0c, 1)

            def scale_rows(t):
                v.wait_ge(s_rb, 2 * DMA * (t.n + 1))
                wait(v, s_xhi, t.n)
                wait(v, s_xlo, t.n)
                order = "p b (s w) -> p s b w"
                v.tensor_tensor(xr[:, :, :, :], xin[:, t.par, :, :].rearrange(order, w=W),
                                rb[:, :, :].rearrange(order, w=W), ALU.mult).then_inc(s_xr, 1)

            def lo_rows_of_x(t):
                v.wait_ge(s_xhi, t.n + 1)
                wait(v, s_stk, DMA * NSTK * t.n)
                v.tensor_tensor(x_lo[:, :, :], xr[:, :, :, :].rearrange("p s b w -> p s (b w)"), x_hi[:, :, :],
                                ALU.subtract).then_inc(s_xlo, 1)

            def lo_part(n, slot, par):
                for h in range(2):
                    v.wait_ge(s_hhi, 2 * (n + 1) + h + 1)
                    v.tensor_tensor(h_stk[par][h][lo_rows(h), :, 1:W + 1],
                                    h32[half(h), slot, :].rearrange("p (b w) -> p b w", w=W),
                                    h_stk[par][h][hi_rows(h), :, 1:W + 1], ALU.subtract).then_inc(s_hlo, 1)

            def step(t, i):
                n, par = RT * t.n + i, i % 2
                v.wait_ge(s_so, n + 1)
                wait(v, s_cell, n)
                if not (known(t.n) and n < 2):
                    v.wait_ge(s_x1, n - 1)
                v.tensor_tensor(h32[:, par, :], cell[:, par, :], sg_o[:, :], ALU.mult).then_inc(s_h32, 1)
                lo_part(n, par, 1 - par)
                v.wait_ge(s_sf, n + 1)
                v.tensor_tensor(fc[:, :], sg_f[:, :], cell[:, par, :], ALU.mult).then_inc(s_prod, 1)
                v.wait_ge(s_ig, 2 * n + 2)
                v.tensor_tensor(ig[:, :], sg_i[:, :], th_g[:, :], ALU.mult).then_inc(s_prod, 1)
                v.wait_ge(s_prod, 2 * n + 2)
                v.tensor_tensor(cell[:, 1 - par, :], fc[:, :], ig[:, :], ALU.add).then_inc(s_cell, 1)

            def stats1(t):
                wait(v, s_fin1, 5 * t.n)
                v.wait_ge(s_xtok, 2 * t.n + 2)
                for b in range(B):
                    ins = v.bn_stats(st1[:, b, :], xtok[:, bass.ds(t.n, 1), b, :].rearrange("p t c -> p (t c)"))
                ins.then_inc(s_bn1, 1)
                variances(t, st1, v1, s_bn1, t.n + 1, s_fin1, s_r1, EPS_FFN)

            def keep_r1(t):
                v.wait_ge(s_r1, t.n + 1)
                v.tensor_copy(rfs[:, bass.ds(t.n, 1), :], r1[:, :].unsqueeze(1)).then_inc(s_rfs, 1)
                v.wait_ge(s_r1t, t.n + 1)
                wait(v, s_scr1, DMA * t.n)
                v.tensor_copy(r1t[:, :], ps_r[0:B, 0:TOK]).then_inc(s_r1c, 1)

            def phase(t, first=False, last=False):
                step(t, 0)
                if not last:
                    stats0(t.shift(1))
                step(t, 1)
                if not last:
                    keep_r0t(t.shift(1))
                if not first:
                    stats1(t.shift(-1))
                step(t, 2)
                if not last:
                    scale_rows(t.shift(1))
                if not first:
                    keep_r1(t.shift(-1))
                if not last:
                    lo_rows_of_x(t.shift(1))
                step(t, 3)

            t0, t7 = Tile(0, 0, 0), Tile(NT - 1, (NT - 1) // 2, 1)
            for k in range(QUAD):
                for h in range(2):
                    v.memset(mask[E * k:E * k + E, h:h + 1], float(k % 2 == h)).then_inc(s_mask, 1)
            v.wait_ge(s_wld, 4 * DMA)
            for m in range(2):
                v.tensor_reduce(w_mean[:, m, :], w_rows[:, m, 0, :].rearrange("p (c k) -> p k c", k=3)[:, 0:2, :],
                                AX.X, ALU.add).then_inc(s_wstep, 1)
            v.wait_ge(s_wstep, 2)
            v.tensor_scalar(w_mean[:, :, :], w_mean[:, :, :], 1.0 / C, None, ALU.mult).then_inc(s_wstep, 1)
            v.wait_ge(s_wstep, 3)
            for n in range(5):
                src, tap = (0, n) if n < 2 else (1, n - 2)
                for m in range(2):
                    rows = w_rows[:, m, src, :].rearrange("p (c k) -> p k c", k=3)[:, tap:tap + 1, :] \
                        .to_broadcast([128, 2, C])
                    dst = w_stack[:, m, n, :].rearrange("p (d c) -> p d c", d=2)
                    if src == 0:
                        v.tensor_scalar(dst, rows, w_mean[:, m, tap:tap + 1], None, ALU.subtract).then_inc(s_wstep, 1)
                    else:
                        v.tensor_copy(dst, rows).then_inc(s_wstep, 1)
            for n in range(5):
                v.wait_ge(s_whi, min(n // 2 * 2 + 2, 5))
                v.tensor_tensor(w_lo[:, n, :], psum[4 + n // 2][:, GATES * (n % 2):GATES * (n % 2) + GATES],
                                w_hi[:, n, :], ALU.subtract).then_inc(s_wlo, 1)
            stats0(t0)
            v.wait_ge(s_wld2, (4 + 2 + QUAD + 1) * DMA)
            v.tensor_tensor(b_rows[:, 0, :], b_rows[:, 0, :], b_rows[:, 1, :], ALU.add).then_inc(s_gws, 1)
            v.tensor_reduce(gw_mean[:, :], gw_rows[:, :], AX.X, ALU.add).then_inc(s_gws, 1)
            v.wait_ge(s_gws, 2)
            v.tensor_scalar(gw_mean[:, :], gw_mean[:, :], 1.0 / C, None, ALU.mult).then_inc(s_gws, 1)
            v.wait_ge(s_gws, 3)
            for h in range(2):
                blk = gw_rows[E * h:E * h + E, C * h:C * h + C]
                v.tensor_scalar(blk, blk, gw_mean[E * h:E * h + E, :], None, ALU.subtract).then_inc(s_gws, 1)
            v.wait_ge(s_gwt, 1)
            v.tensor_copy(bias[:, :], ps_lg[:, 448:452]).then_inc(s_wbias, 1)
            v.tensor_copy(gw[:, :], ps_lg[:, 256:256 + 2 * E]).then_inc(s_gwc, 1)
            v.tensor_copy(b2[:, :], ps_lg[0:C, 384:384 + E]).then_inc(s_gwc, 1)
            v.wait_ge(s_init, 4 * DMA)
            lo_part(-1, 1, 0)
            keep_r0t(t0)
            scale_rows(t0)
            lo_rows_of_x(t0)

            phase(t0, first=True)
            with v.Fori(0, (NT - 2) // 2) as k:
                t = Tile(2 * k + 1, k, 1)
                phase(t)
                phase(t.shift(1))
            phase(t7, last=True)
            stats1(t7)
            keep_r1(t7)

            def tokens(g):
                return lg[:, g, :, :].rearrange("p t k -> p (t k)")

            def best(g):
                v.max(top[:, g, :], tokens(g)).then_inc(s_top, 1)
                v.wait_ge(s_top, g + 1)
                v.tensor_tensor(gb_max[:, g:g + 1], top[:, g, 0:1], gbias[:, :], ALU.add).then_inc(s_sub, 1)
                v.wait_ge(s_sub, 2 * g + 1)
                v.tensor_tensor(gb_sub[:, g:g + 1], gbias[:, :], gb_max[:, g:g + 1], ALU.subtract).then_inc(s_sub, 1)

            def pick(g):
                v.wait_ge(s_exp, 2 * g + 2)
                wait(v, s_pick, g - 1)
                v.match_replace(unpicked[g % 2], top_e[:, g, :], tokens(g), 0.0).then_inc(s_unp, 1)
                v.reciprocal(rsum[:, g:g + 1], esum[:, g:g + 1]).then_inc(s_rsum, 1)
                v.wait_ge(s_unp, g + 1)
                v.tensor_tensor(tokens(g), tokens(g), unpicked[g % 2], ALU.subtract).then_inc(s_pick, 1)

            def keep_picks(g):
                wait(v, s_pool, g - 1)
                for k in range(2):
                    v.wait_ge(s_pt, 2 * g + k + 1)
                    scale = rfs[:, 4 * k:4 * k + 4, QUAD * g:QUAD * g + QUAD].unsqueeze(3) \
                        .to_broadcast([128, 4, QUAD, E])
                    v.tensor_tensor(pick_t[:, g % 2, 4 * k:4 * k + 4, :].rearrange("p t (q e) -> p t q e", e=E),
                                    PICK_BANKS[2 * (g % 2) + k][:, :].rearrange("p (t q e) -> p t q e", q=QUAD, e=E),
                                    scale, ALU.mult).then_inc(s_ptm, 1)

            v.wait_ge(s_lgm, NT)
            v.wait_ge(s_x1f, DMA * NT)
            best(0)
            best(1)
            pick(0)
            best(2)
            pick(1)
            keep_picks(0)
            best(3)
            pick(2)
            keep_picks(1)
            pick(3)
            keep_picks(2)
            keep_picks(3)
            v.wait_ge(s_pool, NG)
            v.wait_ge(s_rsum, NG)
            v.tensor_tensor(pooled[:, :, :], psum[2][:, 0:NG * C].rearrange("p (g c) -> p g c", c=C),
                            rsum[:, :].unsqueeze(2).to_broadcast([128, NG, C]), ALU.mult).then_inc(s_pe, 1)
            v.wait_ge(s_mask, 2 * QUAD)
            v.tensor_tensor(rmask[:, :, :], rsum[:, :].unsqueeze(2).to_broadcast([128, NG, 2]),
                            mask[:, :].unsqueeze(1).to_broadcast([128, NG, 2]), ALU.mult).then_inc(s_rsum, 1)
            v.wait_ge(s_pe, 1)
            v.tensor_reduce(pmean[:, :], pooled[:, :, :], AX.X, ALU.add).then_inc(s_pe, 1)
            v.wait_ge(s_pe, 2)
            v.scalar_tensor_tensor(pooled[:, :, :], pmean[:, :].unsqueeze(2).to_broadcast([128, NG, C]), -1.0 / C,
                                   pooled[:, :, :], ALU.mult, ALU.add).then_inc(s_pe, 1)
            for k in range(4):
                v.wait_ge(s_ht, k + 1)
                v.tensor_copy(hid_t[:, 2 * k:2 * k + 2, :, :].rearrange("p q k j -> p (q k j)"), HT_BANKS[k][:, :]) \
                    .then_inc(s_hte, 1)
            v.wait_ge(s_o, 1)
            v.tensor_tensor(o_t[:, :, :], psum[0][0:C, :].rearrange("p (e i) -> p i e", i=B),
                            b2[:, :].unsqueeze(1).to_broadcast([C, B, E]), ALU.add).then_inc(s_oe, 1)
            v.wait_ge(s_ot, 1)
            v.wait_ge(s_rsum, NG + 1)
            v.tensor_tensor(o_blk[:, :, :, :],
                            psum[1][:, 0:NG * C].rearrange("p (g c) -> p g c", c=C).unsqueeze(2)
                            .to_broadcast([128, NG, 2, C]),
                            rmask[:, :, :].unsqueeze(3).to_broadcast([128, NG, 2, C]), ALU.mult).then_inc(s_ob, 1)
            for n in range(2 * NB):
                b, k = n // 2, n % 2
                v.wait_ge(s_y, n + 1)
                if b >= 2 and k == 0:
                    v.wait_ge(s_out[b % 2], 2 * DMA * (b // 2))
                v.tensor_tensor(y[:, b % 2, 512 * k:512 * k + 512], Y_BANKS[n % 4][:, :],
                                x1f[:, b, 4 * k:4 * k + 4, :].rearrange("p t k -> p (t k)"), ALU.add).then_inc(s_ye, 1)

        @block.tensor
        def _(pe):
            def turn(out_, in_, rows):
                return pe.transpose(out_, in_, ident[0:rows, 0:rows])

            def conv_rows(t, i):
                n, par = RT * t.n + i, i % 2
                if i == 0:
                    pe.wait_ge(s_stk, DMA * NSTK * (t.n + 1))
                if not (known(t.n) and n < 2):
                    pe.wait_ge(s_ig, 2 * (n - 1))
                for gate in range(4):
                    bank = (ps_of, ps_ig)[gate // 2][par]
                    cols = slice(COLS * (gate % 2), COLS * (gate % 2) + COLS)
                    first = gate % 2 == 0
                    for tap in range(2):
                        before = i + tap == 0
                        row = (i + tap - 1) % RT
                        for w in (w_hi, w_lo):
                            for h in range(2):
                                x_rows = x_stk[1 - t.par if before else t.par][h]
                                ins = pe.matmul(bank[half(h), cols], w[:, tap, C * GATE_ORDER[gate]:][:, 0:C],
                                                x_rows[:, row, :], start=first, stop=False)
                            first = False
                ins.then_inc(s_conv, 1)

            def conv_state(t, i):
                n, par = RT * t.n + i, i % 2
                pe.wait_ge(s_hlo, 2 * n + 2)
                for gate in range(4):
                    bank = (ps_of, ps_ig)[gate // 2][par]
                    cols = slice(COLS * (gate % 2), COLS * (gate % 2) + COLS)
                    for tap in range(3):
                        for w in (w_hi, w_lo):
                            for h in range(2):
                                ins = pe.matmul(bank[half(h), cols], w[:, 2 + tap, C * GATE_ORDER[gate]:][:, 0:C],
                                                h_stk[par][h][:, :, tap:tap + W], start=False,
                                                stop=gate % 2 == 1 and tap == 2 and w is w_lo)
                    if gate == 1:
                        ins.then_inc(s_gof, 1)
                ins.then_inc(s_gig, 1)

            def turn_in(t):
                pe.wait_ge(s_xin[t.par], 2 * DMA * (t.half + 1))
                for k in range(2):
                    for b in range(4):
                        ins = turn(ps_t[k][:, 128 * b:128 * b + 128], xin[:, t.par, 4 * k + b, :], 128)
                    ins.then_inc(s_p0t, 1)

            def turn_r0(t):
                pe.wait_ge(s_r0, t.n + 1)
                turn(ps_r[0:B, 0:TOK], r0[:, :], 128).then_inc(s_r0t, 1)

            def turn_x1(t):
                pe.wait_ge(s_x1, RT * (t.n + 1))
                for k in range(2):
                    if known(t.n) and t.n > NT - 3:
                        pe.wait_ge(s_xtok, 2 * (t.n - 1) + k + 1)
                    else:
                        pe.wait_ge(s_bn0, 2 * (t.n + 2) + k + 1)
                    for b in range(4):
                        ins = turn(ps_t[k][:, 128 * b:128 * b + 128], x1t[:, t.par, 4 * k + b, :], 128)
                    ins.then_inc(s_ft, 1)

            def logits(t):
                wait(pe, s_lgr, t.n)
                for g in range(NG):
                    for j in range(2):
                        ins = pe.matmul(ps_lg[C * j:C * j + C, TOK * g:TOK * g + TOK], gw[:, :],
                                        x1t[:, t.par, 2 * g + j, :], start=g == 0, stop=g == NG - 1)
                ins.then_inc(s_lg, 1)

            def turn_r1(t):
                pe.wait_ge(s_r1, t.n + 1)
                if known(t.n) and t.n > NT - 3:
                    wait(pe, s_r1c, t.n)
                else:
                    pe.wait_ge(s_r0c, t.n + 3)
                turn(ps_r[0:B, 0:TOK], r1[:, :], 128).then_inc(s_r1t, 1)

            def phase(t, first=False, last=False):
                conv_state(t, 0)
                if not last:
                    turn_in(t.shift(1))
                conv_rows(t, 1)
                conv_state(t, 1)
                if not first:
                    turn_x1(t.shift(-1))
                conv_rows(t, 2)
                if not last:
                    turn_r0(t.shift(1))
                conv_state(t, 2)
                if not first:
                    logits(t.shift(-1))
                conv_rows(t, 3)
                if not first:
                    turn_r1(t.shift(-1))
                conv_state(t, 3)
                if not last:
                    conv_rows(t.shift(1), 0)

            t0, t7 = Tile(0, 0, 0), Tile(NT - 1, (NT - 1) // 2, 1)
            pe.wait_ge(s_const, 9)
            for n in range(5):
                pe.wait_ge(s_wstep, 3 + 2 * n + 2)
                for m in range(2):
                    ins = turn(psum[4 + n // 2][:, GATES * (n % 2) + 128 * m:][:, 0:128], w_stack[:, m, n, :], 128)
                ins.then_inc(s_wt, 1)
            pe.wait_ge(s_wlo, 4)
            turn_in(t0)
            pe.wait_ge(s_wlo, 5)
            pe.wait_ge(s_gws, 5)
            turn(ps_lg[:, 256:256 + 2 * E], gw_rows[:, :], 2 * E)
            turn(ps_lg[0:C, 384:384 + E], b2_rows[:, :], E)
            turn(ps_lg[:, 448:452], b_rows[:, 0, :], 4).then_inc(s_gwt, 1)
            turn_r0(t0)
            conv_rows(t0, 0)
            pe.wait_ge(s_gwc, 2)
            phase(t0, first=True)
            with pe.Fori(0, (NT - 2) // 2) as k:
                t = Tile(2 * k + 1, k, 1)
                phase(t)
                phase(t.shift(1))
            phase(t7, last=True)
            turn_x1(t7)
            logits(t7)
            turn_r1(t7)

            def turn_picks(g):
                pe.wait_ge(s_pick, g + 1)
                wait(pe, s_ptm, 2 * (g - 1))
                for k in range(2):
                    for m in range(4):
                        ins = turn(PICK_BANKS[2 * (g % 2) + k][:, 128 * m:128 * m + 128], lg[:, g, 4 * k + m, :], 128)
                    ins.then_inc(s_pt, 1)

            def pool(g):
                pe.wait_ge(s_ptm, 2 * g + 2)
                for m in range(NT):
                    for k in range(QUAD):
                        ins = pe.matmul(psum[2][E * k:E * k + E, C * g:C * g + C], pick_t[:, g % 2, m, E * k:E * k + E],
                                        xtok[:, m, QUAD * g + k, :], start=g + m == 0,
                                        stop=g == NG - 1 and m == NT - 1)
                ins.then_inc(s_pool, 1)

            turn_picks(0)
            for g in range(NG):
                if g + 1 < NG:
                    turn_picks(g + 1)
                pool(g)
            pe.wait_ge(s_pe, 3)
            for g in range(NG):
                ins = turn(psum[3][0:C, 128 * g:128 * g + 128], pooled[:, g, :], 128)
            ins.then_inc(s_po, 1)
            pe.wait_ge(s_w12, 3 * DMA)
            pe.wait_ge(s_pot, 1)
            for k in range(4):
                for m in range(2):
                    for j in range(QUAD):
                        e = QUAD * (2 * k + m) + j
                        ins = pe.matmul(HID_BANKS[k][E * j:E * j + E, H * m:H * m + H], pool_t[:, e, :], w1s[:, e, :],
                                        start=m == 0, stop=m == 1)
                ins.then_inc(s_hid, 1)
            for k in range(4):
                pe.wait_ge(s_gelu, k + 1)
                for m in range(4):
                    ins = turn(HT_BANKS[k][:, 128 * m:128 * m + 128],
                               hid[:, 2 * k + m // 2, 128 * (m % 2):128 * (m % 2) + 128], 128)
                ins.then_inc(s_ht, 1)
            for e in range(E):
                if e % 8 == 0:
                    pe.wait_ge(s_hte, e // 8 + 1)
                for k in range(2):
                    ins = pe.matmul(psum[0][0:C, B * e:B * e + B], w2s[:, k, e, :],
                                    hid_t[:, e // QUAD, k, E * (e % QUAD):E * (e % QUAD) + B],
                                    start=e + k == 0, stop=e == E - 1 and k == 1)
            ins.then_inc(s_o, 1)
            pe.wait_ge(s_oe, 1)
            for g in range(NG):
                ins = turn(psum[1][:, C * g:C * g + C],
                           o_t[:, QUAD * g:QUAD * g + QUAD, :].rearrange("p i e -> p (i e)"), C)
            ins.then_inc(s_ot, 1)
            pe.wait_ge(s_ob, 1)
            for n in range(2 * NB):
                b, k = n // 2, n % 2
                g, j = b // 2, b % 2
                wait(pe, s_ye, n - 3)
                pe.matmul(Y_BANKS[n % 4][:, :], o_blk[C * j:C * j + C, g, :, :].rearrange("p h c -> p (h c)"),
                          lg[C * j:C * j + C, g, 4 * k:4 * k + 4, :].rearrange("p t k -> p (t k)"),
                          start=True, stop=True).then_inc(s_y, 1)


_INS = ["x", "L0_conv_w_itos", "L0_conv_b_itos", "L0_conv_w_stos", "L0_conv_b_stos", "L0_conv_h0", "L0_conv_c0",
        "L0_ffn_gate_w", "L0_ffn_gate_b", "L0_ffn_weight1", "L0_ffn_weight2"]


def kernel(**inputs):
    import numpy as np
    import concourse.bacc as bacc
    from concourse.bass_utils import run_bass_kernel_spmd

    nc = bacc.Bacc("TRN2", target_bir_lowering=False, num_devices=1)
    arrays, args = {}, []
    for name in _INS:
        a = np.ascontiguousarray(inputs[name])
        arrays[f"in_{name}"] = a
        args.append(nc.dram_tensor(f"in_{name}", a.shape, F32, kind="ExternalInput").ap())
    args.append(nc.dram_tensor("out", (B, C, S, W), F32, kind="ExternalOutput").ap())
    args += [nc.dram_tensor(f"scratch{k}", (B, TOK), F32, kind="Internal").ap() for k in range(2)]
    metaformer(nc, *args)
    got = run_bass_kernel_spmd(nc, [arrays], core_ids=[0])
    return got.results[0]["out"]
```

```python
from contextlib import ExitStack

import concourse.bass as bass
from concourse import mybir

F32 = mybir.dt.float32
F16 = mybir.dt.float16
ACT = mybir.ActivationFunctionType
ALU = mybir.AluOpType
AX = mybir.AxisListType

B, C, S, W = 16, 64, 32, 32
E, K, H = 32, 8, 256
NB = B // 2
COLS = NB * W
RT = 4
TOK = RT * W
NT = S // RT
NG = NB // 2
QUAD = 4
GATES = 4 * C
GATE_ORDER = (3, 2, 0, 1)
PAD = W + 2
W_STACKS = ((0, 0, 0), (0, 1, 1), (1, 0, 0), (1, 1, 1), (1, 2, 2), (0, 0, 1), (1, 0, 1))
X_PARTS, H_PARTS, X_PAIR, H_PAIR = (0, 1), (2, 3, 4), 5, 6
EPS_CONV, EPS_FFN = 1e-6, 1e-5
YS = 4
DMA = 16
BN = 6
X_LOADS = ((0, 1), (1, 2), (2, 4), (4, 8))
AHEAD = 3


class Tile:

    def __init__(self, n, half, par):
        self.n, self.half, self.par = n, half, par

    def shift(self, d):
        p = self.par + d
        return Tile(self.n + d, self.half + p // 2, p % 2)


def known(v):
    return isinstance(v, int)


def wait(eng, sem, value):
    if not known(value) or value > 0:
        eng.wait_ge(sem, value)


def metaformer(nc, x, w_itos, b_itos, w_stos, b_stos, h0, c0, gate_w, gate_b, w1, w2, out, scratch0, scratch1):
    ctx = ExitStack()
    with ctx:
        def sb(name, shape, dt=F32):
            return ctx.enter_context(nc.sbuf_tensor(name, shape, dt))

        def sem(name):
            return ctx.enter_context(nc.semaphore(name))

        ident = sb("ident", [128, 128])
        w_rows = sb("w_rows", [128, 2, 2, 3 * C])
        w_mean = sb("w_mean", [128, 2, 2])
        w_stack = sb("w_stack", [128, 2, len(W_STACKS), 128])
        w_hi = sb("w_hi", [128, len(W_STACKS), GATES], F16)
        w_lo = sb("w_lo", [128, len(W_STACKS), GATES], F16)
        b_rows = sb("b_rows", [4, 2, 2 * C])
        bias = sb("bias", [128, 4])
        gw_rows = sb("gw_rows", [2 * E, 2 * C])
        gw_mean = sb("gw_mean", [2 * E, 1])
        gw = sb("gw", [128, 2 * E])
        gbias = sb("gbias", [128, 1])
        pow_exp = sb("pow_exp", [128, B])
        w1s = sb("w1s", [C + 1, E, H])
        w2s = sb("w2s", [128, 2, E, C])
        b2_rows = sb("b2_rows", [E, C])
        b2 = sb("b2", [C, E])
        xc = sb("xc", [128, NB, NT, TOK])
        x_in = sb("x_in", [128, NB, TOK])
        st0 = sb("st0", [128, 2, B, BN])
        v0 = sb("v0", [128, 2, 4, B])
        r0 = sb("r0", [128, 2, B])
        r0t = sb("r0t", [B, 2, TOK])
        rb_xr = sb("rb_xr", [128, 2, NB * TOK])
        rb = rb_xr[:, 0, :].rearrange("p (b t) -> p b t", b=NB)
        xr = rb_xr[:, 1, :].rearrange("p (s b w) -> p s b w", s=RT, b=NB)
        x_stks = sb("x_stks", [128, 2, 2, 2, RT * COLS], F16)
        x_parts = [[x_stks[:, p, h, 0, :].rearrange("p (s c) -> p s c", s=RT) for h in range(2)] for p in range(2)]
        x_pair = [[x_stks[:, p, h, 1, :].rearrange("p (s c) -> p s c", s=RT) for h in range(2)] for p in range(2)]
        h_stk = [[sb(f"h_stk{p}{h}", [128, NB, PAD], F16) for h in range(2)] for p in range(2)]
        h_pair = [[sb(f"h_pair{p}{h}", [128, NB, PAD], F16) for h in range(2)] for p in range(2)]
        sg_o = sb("sg_o", [128, COLS])
        sg_f = sb("sg_f", [128, COLS])
        sg_i = sb("sg_i", [128, COLS])
        th_g = sb("th_g", [128, COLS])
        h32 = sb("h32", [128, 2, COLS])
        cell = sb("cell", [128, 2, COLS])
        fc = sb("fc", [128, COLS])
        ig = sb("ig", [128, COLS])
        x1t = sb("x1t", [128, 2, NB, TOK])
        xtok = sb("xtok", [128, NT, B, C])
        st1 = sb("st1", [128, B, BN])
        v1 = sb("v1", [128, 4, B])
        r1 = sb("r1", [128, B])
        r1t = sb("r1t", [B, TOK])
        rbf = sb("rbf", [128, NG, TOK])
        lgr = sb("lgr", [128, NG, TOK])
        lg = sb("lg", [128, NG, NT, TOK])
        top = sb("top", [128, NG, K])
        top_e = sb("top_e", [128, NG, K])
        gb_max = sb("gb_max", [128, NG])
        gb_sub = sb("gb_sub", [128, NG])
        esum = sb("esum", [128, NG])
        rsum = sb("rsum", [128, NG])
        pooled = sg_o[:, :].rearrange("p (g c) -> p g c", c=C)
        pmean = sb("pmean", [128, NG])
        mask = sb("mask", [128, QUAD])
        rmask = sb("rmask", [128, NG, QUAD])
        tail_room = x_stks[:, :, :, :, :].rearrange("p a b c k -> p (a b c k)").bitcast(F32)
        unpicked = [tail_room[:, NT * TOK * g:NT * TOK * g + NT * TOK] for g in range(NG)]
        y = tail_room.rearrange("p (a k) -> p a k", a=YS)
        hid = xtok[:, 0:2, :, :].rearrange("p a b c -> p (a b c)").rearrange("p (q h) -> p q h", h=H)
        hid_t = rb_xr[:, :, :].rearrange("p a (q k j) -> p (a q) k j", k=2, j=128)
        pool_t = w_stack[0:C + 1, :, :, :].rearrange("p a n k -> p (a n k)")[:, 0:2 * B * E] \
            .rearrange("p (e i) -> p e i", e=E)
        o_img = h32[:, :, :].rearrange("p a k -> p (a k)")
        o_t = lgr[0:C, :, :].rearrange("p g (i e) -> p (g i) e", e=E)
        o_blk = x1t[:, 0, :, :].rearrange("p b k -> p (b k)").rearrange("p (g q c) -> p g q c", g=NG, q=QUAD)
        pick_t = x1t[:, :, :, :]

        psum = [ctx.enter_context(nc.psum_tensor(f"ps{i}", [128, 512], F32)) for i in range(8)]
        ps_of, ps_ig = psum[0:2], psum[2:4]
        ps_t = psum[4:6]
        ps_lg, ps_r = psum[6], psum[7]
        PICK_BANKS = psum[4:6] + psum[0:2]
        HID_BANKS = psum[0:2] + psum[4:6]
        HT_BANKS = psum[2:4] + psum[6:8]
        OT_BANKS = (psum[1], psum[4])
        OB_BANK = psum[5]
        Y_BANKS = psum[6:8] + psum[2:4] + psum[0:2] + psum[4:6]

        s_const = sem("s_const")
        s_const2 = sem("s_const2")
        s_wld = sem("s_wld")
        s_wld2 = sem("s_wld2")
        s_mask = sem("s_mask")
        s_wbias = sem("s_wbias")
        s_gws = sem("s_gws")
        s_gwt = sem("s_gwt")
        s_gwc = sem("s_gwc")
        s_lgr = sem("s_lgr")
        s_rsum = sem("s_rsum")
        s_wstep = sem("s_wstep")
        s_wt = sem("s_wt")
        s_whi = sem("s_whi")
        s_wlo = sem("s_wlo")
        s_w12 = sem("s_w12")
        s_zero = sem("s_zero")
        s_init = sem("s_init")
        s_x = [sem(f"s_xload{n}") for n in range(len(X_LOADS))]
        s_hpair = sem("s_hpair")
        s_p0t = sem("s_p0t")
        s_bn0 = sem("s_bn0")
        s_fin0 = sem("s_fin0")
        s_r0 = sem("s_r0")
        s_r0t = sem("s_r0t")
        s_r0c = sem("s_r0c")
        s_scr0 = sem("s_scr0")
        s_rb = sem("s_rb")
        s_xr = sem("s_xr")
        s_xhi = sem("s_xhi")
        s_xlo = [sem(f"s_xlo{h}") for h in range(2)]
        s_xin = sem("s_xin")
        s_xs = sem("s_xs")
        s_xst = sem("s_xst")
        s_stk = sem("s_stk")
        s_conv = sem("s_conv")
        s_gof = sem("s_gof")
        s_gig = sem("s_gig")
        s_so = sem("s_so")
        s_sf = sem("s_sf")
        s_ig = sem("s_ig")
        s_h32 = sem("s_h32")
        s_hhi = sem("s_hhi")
        s_hlo = sem("s_hlo")
        s_cell = sem("s_cell")
        s_prod = sem("s_prod")
        s_x1 = sem("s_x1")
        s_x1f = sem("s_x1f")
        s_ft = sem("s_ft")
        s_xtok = sem("s_xtok")
        s_bn1 = sem("s_bn1")
        s_fin1 = sem("s_fin1")
        s_r1 = sem("s_r1")
        s_xts = sem("s_xts")
        s_rb1 = sem("s_rb1")
        s_r1t = sem("s_r1t")
        s_r1c = sem("s_r1c")
        s_scr1 = sem("s_scr1")
        s_rbf = sem("s_rbf")
        s_lg = sem("s_lg")
        s_lgm = sem("s_lgm")
        s_lgm7 = sem("s_lgm7")
        s_top = sem("s_top")
        s_sub = sem("s_sub")
        s_exp = sem("s_exp")
        s_tope = sem("s_tope")
        s_unp = sem("s_unp")
        s_pick = [sem(f"s_pick{g}") for g in range(NG)]
        s_pt = sem("s_pt")
        s_ptm = sem("s_ptm")
        s_pool = sem("s_pool")
        s_pe = sem("s_pe")
        s_po = sem("s_po")
        s_pot = sem("s_pot")
        s_hid = sem("s_hid")
        s_gelu = sem("s_gelu")
        s_ht = sem("s_ht")
        s_hte = sem("s_hte")
        s_o = sem("s_o")
        s_oe = sem("s_oe")
        s_ot = sem("s_ot")
        s_ob = sem("s_ob")
        s_y = sem("s_y")
        s_ye = sem("s_ye")
        s_oi = sem("s_oi")
        s_oie = sem("s_oie")
        s_out = [sem(f"s_out{p}") for p in range(YS)]

        x_cm = x.rearrange("(a b) c s w -> a c b (s w)", a=2)
        out_cm = out.rearrange("(a b) c s w -> a c b (s w)", a=2)

        NSTK = 6

        def half(h):
            return slice(C * h, C * h + C)

        def hi_rows(h):
            return slice(C * h, C * h + C)

        def lo_rows(h):
            return slice(C * (1 - h), C * (1 - h) + C)

        block = ctx.enter_context(nc.Block())

        @block.sync
        def _(q):
            def load_x_in(t):
                q.wait_ge(s_p0t, 2 * t.n)
                for h in range(2):
                    q.dma_start(x_in[half(h), :, :], x_cm[h, :, :, bass.ds(t.n * TOK, TOK)]).then_inc(s_xin, DMA)

            def store_r0(t):
                q.wait_ge(s_r0c, t.n)
                q.dma_start(scratch0[t.par], r0t[:, t.par, :]).then_inc(s_scr0, DMA)

            def spread_r0(t):
                q.wait_ge(s_scr0, DMA * t.n)
                for h in range(2):
                    q.dma_start(rb[half(h), :, :], scratch0[t.par].rearrange("(b h) t -> h b t", h=2)[h]
                                .partition_broadcast(C)).then_inc(s_rb, DMA)

            def stack_x(t):
                for h in range(2):
                    q.wait_ge(s_xhi, 2 * t.n + h + 1)
                    hi = x_parts[t.par][h][hi_rows(h), :, :]
                    pair, below = x_pair[t.par][h], x_pair[1 - t.par][h]
                    q.dma_start(pair[0:C, 1:RT, :], hi[:, 0:RT - 1, :]).then_inc(s_stk, DMA)
                    q.dma_start(pair[C:2 * C, :, :], hi).then_inc(s_stk, DMA)
                    q.dma_start(below[0:C, 0:1, :], hi[:, RT - 1:RT, :]).then_inc(s_stk, DMA)

            def spread_r1(t):
                q.wait_ge(s_r1c, t.n + 1)
                q.dma_start(scratch1[:, :], r1t[:, :]).then_inc(s_scr1, DMA)
                q.wait_ge(s_scr1, DMA * (t.n + 1))
                r_g = scratch1.rearrange("(g q) t -> q g t", q=QUAD)
                for k in range(QUAD):
                    q.dma_start(rbf[E * k:E * k + E, :, :], r_g[k].partition_broadcast(E)).then_inc(s_rbf, DMA)

            def keep_x1(t):
                q.wait_ge(s_x1, RT * (t.n + 1))
                q.dma_start(xc[:, :, bass.ds(t.n, 1), :], x1t[:, t.par, :, :].unsqueeze(2)).then_inc(s_x1f, DMA)

            def phase(t, first=False, left=AHEAD):
                if not first and left >= AHEAD:
                    load_x_in(t.shift(AHEAD))
                if not first:
                    keep_x1(t.shift(-1))
                if left > 0:
                    stack_x(t.shift(1))
                if left > 1:
                    store_r0(t.shift(2))
                    spread_r0(t.shift(2))
                if not first:
                    spread_r1(t.shift(-1))

            t0, t7 = Tile(0, 0, 0), Tile(NT - 1, (NT - 1) // 2, 1)
            def load_x(k):
                a, b = X_LOADS[k]
                for h in range(2):
                    q.dma_start(xc[half(h), :, a:b, :], x_cm[h, :, :, a * TOK:b * TOK]
                                .rearrange("c b (n t) -> c b n t", t=TOK)).then_inc(s_x[k], DMA)

            load_x(0)
            for a in range(2):
                for n, w in enumerate((w_itos, w_stos)):
                    q.dma_start(w_rows[:, a, n, :], w[128 * a:128 * a + 128].rearrange("o c k one -> o (c k one)")) \
                        .then_inc(s_wld, DMA)
            load_x(1)
            for h in range(2):
                q.dma_start(h32[half(h), 1, :].rearrange("p (b w) -> p b w", w=W),
                            h0.rearrange("c w one -> c one w").to_broadcast([C, NB, W])).then_inc(s_init, DMA)
                q.dma_start(cell[half(h), 0, :].rearrange("p (b w) -> p b w", w=W),
                            c0.rearrange("c w one -> c one w").to_broadcast([C, NB, W])).then_inc(s_init, DMA)
            for h in range(2):
                for n, b in enumerate((b_itos, b_stos)):
                    q.dma_start(b_rows[:, n, half(h)], b.rearrange("(g c) -> g c", c=C)).then_inc(s_wld2, DMA)
            load_x(2)
            q.wait_ge(s_zero, 1)
            for h in range(2):
                q.dma_start(gw_rows[E * h:E * h + E, C * h:C * h + C], gate_w).then_inc(s_wld2, DMA)
            for k in range(QUAD):
                q.dma_start(gbias[E * k:E * k + E, :], gate_b.unsqueeze(1)).then_inc(s_wld2, DMA)
            q.dma_start(b2_rows[:, :], w2[:, H, :]).then_inc(s_wld2, DMA)
            stack_x(t0)
            store_r0(t0.shift(1))
            spread_r0(t0.shift(1))
            load_x(3)
            phase(t0, first=True)
            with q.Fori(0, (NT - 4) // 2) as k:
                t = Tile(2 * k + 1, k, 1)
                phase(t)
                phase(t.shift(1))
            for left in (2, 1, 0):
                phase(t7.shift(-left), left=left)
            keep_x1(t7)
            q.dma_start(w1s[:, :, :], w1.rearrange("e k h -> k e h")).then_inc(s_w12, DMA)
            for k in range(2):
                q.dma_start(w2s[:, k, :, :], w2[:, 128 * k:128 * k + 128, :].rearrange("e k o -> k e o")) \
                    .then_inc(s_w12, DMA)
            for b in range(NB):
                q.wait_ge(s_ye, 2 * b + 2)
                for h in range(2):
                    q.dma_start(out_cm[h, :, b, :], y[half(h), b % YS, :]).then_inc(s_out[b % YS], DMA)
            for p in range(YS):
                q.wait_ge(s_out[p], 2 * DMA * NB // YS)

        @block.gpsimd
        def _(p):
            p.memset(gw_rows[:, :], 0.0).then_inc(s_zero, 1)
            p.memset(ident[:, :], 0.0).then_inc(s_const, 1)
            p.wait_ge(s_const, 1)
            p.affine_select(out=ident[:, :], in_=ident[:, :], compare_op=ALU.not_equal, fill=1.0,
                            base=0, pattern=[[-1, 128]], channel_multiplier=1).then_inc(s_const, 1)
            p.memset(pow_exp[:, :], -0.5).then_inc(s_const, 1)
            for par in range(2):
                for h in range(2):
                    p.memset(h_stk[par][h][:, :, :], 0.0).then_inc(s_const, 1)
                    p.memset(h_pair[par][h][:, :, :], 0.0).then_inc(s_const, 1)
            for h in range(2):
                p.memset(x_parts[1][h][:, RT - 1, :], 0.0).then_inc(s_const, 1)
                p.memset(x_pair[0][h][0:C, 0, :], 0.0).then_inc(s_const, 1)
            p.wait_ge(s_const, 15)

            def rsqrt0(t):
                p.wait_ge(s_fin0, 5 * (t.n + 1))
                if known(t.n) and t.n == 2:
                    p.wait_ge(s_xs, 2)
                elif not known(t.n) or t.n > 2:
                    p.wait_ge(s_r0t, t.n - 2)
                p.tensor_tensor(r0[:, t.par, :], v0[:, t.par, 1, :], pow_exp[:, :], ALU.pow).then_inc(s_r0, 1)

            def rsqrt1(t):
                p.wait_ge(s_fin1, 5 * (t.n + 1))
                p.tensor_tensor(r1[:, :], v1[:, 1, :], pow_exp[:, :], ALU.pow).then_inc(s_r1, 1)

            def scale_tokens(t):
                p.wait_ge(s_r1, t.n + 1)
                here = xtok[:, bass.ds(t.n, 1), :, :].rearrange("p t b c -> p (t b) c")
                p.tensor_tensor(here, here, r1[:, :].unsqueeze(2).to_broadcast([128, B, C]), ALU.mult) \
                    .then_inc(s_xts, 1)

            def residual(t, i):
                n = RT * t.n + i
                p.wait_ge(s_h32, n + 1)
                rows = slice(W * i, W * i + W)
                p.tensor_tensor(x1t[:, t.par, :, rows].unsqueeze(2), xc[:, :, bass.ds(t.n, 1), rows],
                                h32[:, i % 2, :].rearrange("p (b w) -> p b w", w=W).unsqueeze(2), ALU.add) \
                    .then_inc(s_x1, 1)

            def scale_logits(t):
                p.wait_ge(s_lgr, t.n + 1)
                p.wait_ge(s_rbf, QUAD * DMA * (t.n + 1))
                p.tensor_tensor(lg[:, :, bass.ds(t.n, 1), :], lgr[:, :, :].unsqueeze(2), rbf[:, :, :].unsqueeze(2),
                                ALU.mult).then_inc(s_lgm, 1)

            def scale_rows(t, before):
                p.wait_ge(s_rb, 2 * DMA * t.n)
                for h in range(2):
                    p.wait_ge(s_xlo[h], t.n)
                p.tensor_tensor(xr[:, :, :, :],
                                xc[:, :, 1:, :][:, :, bass.ds(before, 1), :]
                                .rearrange("p b n (s w) -> p (n s) b w", w=W),
                                rb[:, :, :].rearrange("p b (s w) -> p s b w", w=W), ALU.mult).then_inc(s_xr, 1)

            def lo_of_x(t):
                p.wait_ge(s_xhi, 2 * t.n + 1)
                p.tensor_tensor(x_parts[t.par][0][lo_rows(0), :, :],
                                xr[half(0), :, :, :].rearrange("p s b w -> p s (b w)"),
                                x_parts[t.par][0][hi_rows(0), :, :], ALU.subtract).then_inc(s_xlo[0], 1)

            def phase(t, first=False, left=AHEAD):
                residual(t, 0)
                if left > 0:
                    scale_rows(t.shift(1), t.n)
                residual(t, 1)
                if not first:
                    rsqrt1(t.shift(-1))
                if left > 0:
                    if first:
                        p.wait_ge(s_x1, 2)
                    else:
                        p.wait_ge(s_r1, t.n)
                    lo_of_x(t.shift(1))
                    p.wait_ge(s_xlo[0], t.n + 2)
                residual(t, 2)
                if not first:
                    scale_tokens(t.shift(-1))
                residual(t, 3)
                if left >= AHEAD:
                    rsqrt0(t.shift(AHEAD))
                if not first:
                    p.wait_ge(s_x1f, DMA * t.n)
                    scale_logits(t.shift(-1))

            t0, t7 = Tile(0, 0, 0), Tile(NT - 1, (NT - 1) // 2, 1)
            rsqrt0(t0)
            rsqrt0(t0.shift(1))
            rsqrt0(t0.shift(2))
            p.wait_ge(s_wt, len(W_STACKS))
            p.memset(pool_t[:, :, :], 0.0).then_inc(s_const2, 1)
            p.wait_ge(s_const2, 1)
            p.memset(pool_t[C:C + 1, :, :], 1.0).then_inc(s_const2, 1)
            p.wait_ge(s_const2, 2)
            phase(t0, first=True)
            p.wait_ge(s_x[-1], 2 * DMA)
            with p.Fori(0, (NT - 4) // 2) as k:
                t = Tile(2 * k + 1, k, 1)
                phase(t)
                phase(t.shift(1))
            for left in (2, 1, 0):
                phase(t7.shift(-left), left=left)
            rsqrt1(t7)
            scale_tokens(t7)
            for g in range(NG - 1):
                p.wait_ge(s_unp, g + 1)
                tokens = lg[:, g, :, :].rearrange("p t k -> p (t k)")
                p.tensor_tensor(tokens, tokens, unpicked[g], ALU.subtract).then_inc(s_pick[g], 1)

        @block.scalar
        def _(a):
            def hi_of_x0():
                for h in range(2):
                    for k in range(2):
                        a.wait_ge(s_xst, k + 1)
                        ins = a.activation(x_parts[0][h][hi_rows(h), :, 4 * W * k:4 * W * k + 4 * W]
                                           .rearrange("p s (b w) -> p s b w", w=W),
                                           ps_t[k][half(h), :].rearrange("p (b s w) -> p s b w", s=RT, w=W), ACT.Copy)
                    ins.then_inc(s_xhi, 1)

            def hi_of_x(t):
                a.wait_ge(s_conv, RT * t.n - 3)
                for h in range(2):
                    a.wait_ge(s_xr, t.n)
                    a.activation(x_parts[t.par][h][hi_rows(h), :, :],
                                 xr[half(h), :, :, :].rearrange("p s b w -> p s (b w)"), ACT.Copy).then_inc(s_xhi, 1)

            def hi_part(n, slot, par):
                for h in range(2):
                    a.activation(h_stk[par][h][hi_rows(h), :, 1:W + 1],
                                 h32[half(h), slot, :].rearrange("p (b w) -> p b w", w=W), ACT.Copy) \
                        .then_inc(s_hhi, 1)

            def step(t, i, between=None):
                n, par = RT * t.n + i, i % 2
                a.wait_ge(s_gof, n + 1)
                wait(a, s_h32, n)
                a.activation(sg_o[:, :], ps_of[par][:, 0:COLS], ACT.Sigmoid, bias=bias[:, 3:4]).then_inc(s_so, 1)
                wait(a, s_cell, n)
                a.activation(sg_f[:, :], ps_of[par][:, COLS:2 * COLS], ACT.Sigmoid, bias=bias[:, 2:3]) \
                    .then_inc(s_sf, 1)
                a.wait_ge(s_h32, n + 1)
                hi_part(n, par, 1 - par)
                if between:
                    keep_tokens(between)
                a.wait_ge(s_gig, n + 1)
                a.activation(sg_i[:, :], ps_ig[par][:, 0:COLS], ACT.Sigmoid, bias=bias[:, 0:1]).then_inc(s_ig, 1)
                a.activation(th_g[:, :], ps_ig[par][:, COLS:2 * COLS], ACT.Tanh, bias=bias[:, 1:2]) \
                    .then_inc(s_ig, 1)

            def keep_tokens(t):
                for k in range(2):
                    a.wait_ge(s_ft, 2 * t.n + k + 1)
                    a.activation(xtok[:, bass.ds(t.n, 1), 8 * k:8 * k + 8, :].rearrange("p t b c -> p t (b c)"),
                                 ps_t[k][:, :].unsqueeze(1), ACT.Copy).then_inc(s_xtok, 1)

            def keep_logits(t):
                a.wait_ge(s_lg, t.n + 1)
                a.activation(lgr[:, :, :].rearrange("p g t -> p (g t)"), ps_lg[:, :], ACT.Copy).then_inc(s_lgr, 1)

            def phase(t, first=False, left=AHEAD):
                step(t, 0, between=None if first else t.shift(-1))
                step(t, 1)
                if left > 0:
                    hi_of_x(t.shift(1))
                step(t, 2)
                if not first:
                    keep_logits(t.shift(-1))
                step(t, 3)

            hi_of_x0()
            for n in range(len(W_STACKS)):
                a.wait_ge(s_wt, min(n // 2 * 2 + 2, len(W_STACKS)))
                a.activation(w_hi[:, n, :], psum[n // 2][:, GATES * (n % 2):GATES * (n % 2) + GATES], ACT.Copy) \
                    .then_inc(s_whi, 1)
            a.wait_ge(s_init, 4 * DMA)
            a.wait_ge(s_const, 11)
            hi_part(-1, 1, 0)
            t0, t7 = Tile(0, 0, 0), Tile(NT - 1, (NT - 1) // 2, 1)
            a.wait_ge(s_wbias, 1)
            phase(t0, first=True)
            with a.Fori(0, (NT - 4) // 2) as k:
                t = Tile(2 * k + 1, k, 1)
                phase(t)
                phase(t.shift(1))
            for left in (2, 1, 0):
                phase(t7.shift(-left), left=left)
            keep_tokens(t7)
            a.wait_ge(s_lgm, NT - 1)
            keep_logits(t7)

            def exponentials(g):
                a.wait_ge(s_sub, 2 * g + 2)
                tokens = lg[:, g, :, :].rearrange("p t k -> p (t k)")
                a.activation(tokens, tokens, ACT.Exp, bias=gb_sub[:, g:g + 1], accum_out=esum[:, g:g + 1]) \
                    .then_inc(s_exp, 1)
                a.activation(top_e[:, g, :], top[:, g, :], ACT.Exp, bias=gb_sub[:, g:g + 1]).then_inc(s_exp, 1)

            def keep_picks(g):
                if g == 0:
                    a.wait_ge(s_x1f, DMA * NT)
                if g > 1:
                    a.wait_ge(s_pool, g - 1)
                for k in range(2):
                    a.wait_ge(s_pt, 2 * g + k + 1)
                    a.activation(pick_t[:, g % 2, 4 * k:4 * k + 4, :].rearrange("p t e -> p (t e)"),
                                 PICK_BANKS[2 * (g % 2) + k][:, :], ACT.Copy).then_inc(s_ptm, 1)

            exponentials(0)
            exponentials(1)
            exponentials(2)
            keep_picks(0)
            exponentials(3)
            for g in range(1, NG):
                keep_picks(g)
            a.wait_ge(s_po, 1)
            a.wait_ge(s_const2, 2)
            a.activation(pool_t[0:C, :, 0:B], psum[3][0:C, :].rearrange("p (i e) -> p e i", e=E), ACT.Copy) \
                .then_inc(s_pot, 1)
            for k in range(4):
                a.wait_ge(s_hid, k + 1)
                a.activation(hid[:, 2 * k:2 * k + 2, :].rearrange("p q h -> p (q h)"), HID_BANKS[k][:, :], ACT.Gelu) \
                    .then_inc(s_gelu, 1)
            a.wait_ge(s_oi, 1)
            a.activation(o_img[:, :], psum[0][:, :], ACT.Copy).then_inc(s_oie, 1)

        @block.vector
        def _(v):
            def variances(t, st, var, s_bn, count, s_fin, eps):
                v.wait_ge(s_bn, count)
                v.tensor_tensor(var[:, 0, :], st[:, :, 1], st[:, :, 4], ALU.subtract).then_inc(s_fin, 1)
                v.tensor_scalar(var[:, 1, :], st[:, :, 2], 1.0 / C, eps, ALU.mult, ALU.add).then_inc(s_fin, 1)
                v.wait_ge(s_fin, 5 * t.n + 2)
                v.scalar_tensor_tensor(var[:, 2, :], var[:, 0, :], 0.25, var[:, 0, :], ALU.mult, ALU.mult) \
                    .then_inc(s_fin, 1)
                v.scalar_tensor_tensor(var[:, 3, :], st[:, :, 5], 1.0 / C, var[:, 1, :], ALU.mult, ALU.add) \
                    .then_inc(s_fin, 1)
                v.wait_ge(s_fin, 5 * t.n + 4)
                v.tensor_tensor(var[:, 1, :], var[:, 2, :], var[:, 3, :], ALU.add).then_inc(s_fin, 1)

            def stats0(t, banks):
                for k in range(2):
                    if k == 0 and (not known(t.n) or t.n > 1):
                        v.wait_ge(s_r0, t.n - 1)
                    v.wait_ge(s_p0t, 2 * t.n + k + 1)
                    for b in range(8):
                        ins = v.bn_stats(st0[:, t.par, 8 * k + b, :], banks[k][:, C * b:C * b + C])
                    ins.then_inc(s_bn0, 1)

            def variances0(t):
                variances(t, st0[:, t.par, :, :], v0[:, t.par, :, :], s_bn0, 2 * t.n + 2, s_fin0, EPS_CONV)

            def scale_tokens0():
                v.wait_ge(s_r0, 1)
                for k in range(2):
                    v.tensor_tensor(xtok[:, 0, 8 * k:8 * k + 8, :], ps_t[k][:, :].rearrange("p (b c) -> p b c", c=C),
                                    r0[:, 0, 8 * k:8 * k + 8].unsqueeze(2).to_broadcast([128, 8, C]), ALU.mult) \
                        .then_inc(s_xs, 1)

            def keep_r0t(t):
                v.wait_ge(s_r0t, t.n)
                if not known(t.n) or t.n > 2:
                    v.wait_ge(s_scr0, DMA * (t.n - 2))
                v.tensor_copy(r0t[:, t.par, :], ps_r[0:B, 0:TOK]).then_inc(s_r0c, 1)

            def lo_of_x0():
                for h in range(2):
                    v.wait_ge(s_xhi, h + 1)
                    for k in range(2):
                        cols = slice(4 * W * k, 4 * W * k + 4 * W)
                        ins = v.tensor_tensor(x_parts[0][h][lo_rows(h), :, cols].rearrange("p s (b w) -> p s b w", w=W),
                                              ps_t[k][half(h), :].rearrange("p (b s w) -> p s b w", s=RT, w=W),
                                              x_parts[0][h][hi_rows(h), :, cols]
                                              .rearrange("p s (b w) -> p s b w", w=W), ALU.subtract)
                    ins.then_inc(s_xlo[h], 1)

            def lo_of_x(t):
                v.wait_ge(s_xhi, 2 * t.n + 2)
                v.tensor_tensor(x_parts[t.par][1][lo_rows(1), :, :],
                                xr[half(1), :, :, :].rearrange("p s b w -> p s (b w)"),
                                x_parts[t.par][1][hi_rows(1), :, :], ALU.subtract).then_inc(s_xlo[1], 1)

            def lo_part(n, slot, par):
                for h in range(2):
                    v.wait_ge(s_hhi, 2 * (n + 1) + h + 1)
                    v.tensor_tensor(h_stk[par][h][lo_rows(h), :, 1:W + 1],
                                    h32[half(h), slot, :].rearrange("p (b w) -> p b w", w=W),
                                    h_stk[par][h][hi_rows(h), :, 1:W + 1], ALU.subtract).then_inc(s_hlo, 1)
                for h in range(2):
                    hi = h_stk[par][h][hi_rows(h), :, 1:W + 1]
                    v.tensor_copy(h_pair[par][h][0:C, :, 1:W + 1], hi).then_inc(s_hpair, 1)
                    v.tensor_copy(h_pair[par][h][C:2 * C, :, 0:W], hi).then_inc(s_hpair, 1)

            def step(t, i):
                n, par = RT * t.n + i, i % 2
                v.wait_ge(s_so, n + 1)
                wait(v, s_cell, n)
                if not (known(t.n) and n < 2):
                    v.wait_ge(s_x1, n - 1)
                v.tensor_tensor(h32[:, par, :], cell[:, par, :], sg_o[:, :], ALU.mult).then_inc(s_h32, 1)
                lo_part(n, par, 1 - par)
                v.wait_ge(s_sf, n + 1)
                v.tensor_tensor(fc[:, :], sg_f[:, :], cell[:, par, :], ALU.mult).then_inc(s_prod, 1)
                v.wait_ge(s_ig, 2 * n + 2)
                v.tensor_tensor(ig[:, :], sg_i[:, :], th_g[:, :], ALU.mult).then_inc(s_prod, 1)
                v.wait_ge(s_prod, 2 * n + 2)
                v.tensor_tensor(cell[:, 1 - par, :], fc[:, :], ig[:, :], ALU.add).then_inc(s_cell, 1)

            def stats1(t):
                v.wait_ge(s_xtok, 2 * t.n + 2)
                for b in range(B):
                    ins = v.bn_stats(st1[:, b, :], xtok[:, bass.ds(t.n, 1), b, :].rearrange("p t c -> p (t c)"))
                ins.then_inc(s_bn1, 1)
                variances(t, st1, v1, s_bn1, t.n + 1, s_fin1, EPS_FFN)

            def keep_r1(t):
                v.wait_ge(s_r1, t.n + 1)
                v.wait_ge(s_r1t, t.n + 1)
                v.tensor_copy(r1t[:, :], ps_r[0:B, 0:TOK]).then_inc(s_r1c, 1)

            def phase(t, first=False, left=AHEAD):
                ahead = t.shift(AHEAD)
                for i in range(RT):
                    step(t, i)
                    if i == 1 and left > 1:
                        keep_r0t(t.shift(2))
                    if i == 0 and not first:
                        stats1(t.shift(-1))
                    if i == 1 and left >= AHEAD:
                        stats0(ahead, ps_t)
                    if i == 2 and not first:
                        keep_r1(t.shift(-1))
                    if i == 2 and left > 0:
                        lo_of_x(t.shift(1))
                    if i == 3 and left >= AHEAD:
                        variances0(ahead)

            t0, t7 = Tile(0, 0, 0), Tile(NT - 1, (NT - 1) // 2, 1)
            for k in range(QUAD):
                for q in range(QUAD):
                    v.memset(mask[E * k:E * k + E, q:q + 1], float(k == q)).then_inc(s_mask, 1)
            for t, banks in ((t0, ps_t), (t0.shift(1), psum[6:8])):
                stats0(t, banks)
                variances0(t)
            scale_tokens0()
            v.wait_ge(s_wld, 4 * DMA)
            for m in range(2):
                v.tensor_reduce(w_mean[:, m, :], w_rows[:, m, 0, :].rearrange("p (c k) -> p k c", k=3)[:, 0:2, :],
                                AX.X, ALU.add).then_inc(s_wstep, 1)
            v.wait_ge(s_wstep, 2)
            v.tensor_scalar(w_mean[:, :, :], w_mean[:, :, :], 1.0 / C, None, ALU.mult).then_inc(s_wstep, 1)
            v.wait_ge(s_wstep, 3)
            for n, (src, *taps) in enumerate(W_STACKS):
                for m in range(2):
                    for d, tap in enumerate(taps):
                        rows = w_rows[:, m, src, tap:3 * C:3]
                        dst = w_stack[:, m, n, C * d:C * d + C]
                        if src == 0:
                            v.tensor_scalar(dst, rows, w_mean[:, m, tap:tap + 1], None, ALU.subtract) \
                                .then_inc(s_wstep, 1)
                        else:
                            v.tensor_copy(dst, rows).then_inc(s_wstep, 1)
            keep_r0t(t0.shift(1))
            lo_of_x0()
            for n in range(len(W_STACKS)):
                v.wait_ge(s_whi, min(n // 2 * 2 + 2, len(W_STACKS)))
                v.tensor_tensor(w_lo[:, n, :], psum[n // 2][:, GATES * (n % 2):GATES * (n % 2) + GATES],
                                w_hi[:, n, :], ALU.subtract).then_inc(s_wlo, 1)
            v.wait_ge(s_wld2, (4 + 2 + QUAD + 1) * DMA)
            v.tensor_tensor(b_rows[:, 0, :], b_rows[:, 0, :], b_rows[:, 1, :], ALU.add).then_inc(s_gws, 1)
            v.tensor_reduce(gw_mean[:, :], gw_rows[:, :], AX.X, ALU.add).then_inc(s_gws, 1)
            v.wait_ge(s_gws, 2)
            v.tensor_scalar(gw_mean[:, :], gw_mean[:, :], 1.0 / C, None, ALU.mult).then_inc(s_gws, 1)
            v.wait_ge(s_gws, 3)
            for h in range(2):
                blk = gw_rows[E * h:E * h + E, C * h:C * h + C]
                v.tensor_scalar(blk, blk, gw_mean[E * h:E * h + E, :], None, ALU.subtract).then_inc(s_gws, 1)
            v.wait_ge(s_gwt, 1)
            v.tensor_copy(bias[:, :], ps_lg[:, 448:452]).then_inc(s_wbias, 1)
            v.tensor_copy(gw[:, :], ps_lg[:, 256:256 + 2 * E]).then_inc(s_gwc, 1)
            v.tensor_copy(b2[:, :], ps_lg[0:C, 384:384 + E]).then_inc(s_gwc, 1)
            v.wait_ge(s_init, 4 * DMA)
            lo_part(-1, 1, 0)
            stats0(t0.shift(2), ps_t)
            variances0(t0.shift(2))
            phase(t0, first=True)
            with v.Fori(0, (NT - 4) // 2) as k:
                t = Tile(2 * k + 1, k, 1)
                phase(t)
                phase(t.shift(1))
            for left in (2, 1, 0):
                phase(t7.shift(-left), left=left)
            stats1(t7)

            def tokens(g):
                return lg[:, g, :, :].rearrange("p t k -> p (t k)")

            def best(g):
                v.max(top[:, g, :], tokens(g)).then_inc(s_top, 1)
                v.wait_ge(s_top, g + 1)
                v.tensor_tensor(gb_max[:, g:g + 1], top[:, g, 0:1], gbias[:, :], ALU.add).then_inc(s_sub, 1)
                v.wait_ge(s_sub, 2 * g + 1)
                v.tensor_tensor(gb_sub[:, g:g + 1], gbias[:, :], gb_max[:, g:g + 1], ALU.subtract).then_inc(s_sub, 1)

            def pick(g):
                v.wait_ge(s_exp, 2 * g + 2)
                v.match_replace(unpicked[g], top_e[:, g, :], tokens(g), 0.0).then_inc(s_unp, 1)
                v.reciprocal(rsum[:, g:g + 1], esum[:, g:g + 1]).then_inc(s_rsum, 1)

            v.wait_ge(s_lgr, NT)
            v.wait_ge(s_rb1, 1)
            v.tensor_tensor(lg[:, :, NT - 1, :], lgr[:, :, :], psum[0][:, :].rearrange("p (g t) -> p g t", t=TOK),
                            ALU.mult).then_inc(s_lgm7, 1)
            v.wait_ge(s_lgm7, 1)
            v.wait_ge(s_lgm, NT - 1)
            best(0)
            best(1)
            pick(0)
            best(2)
            pick(1)
            best(3)
            pick(2)
            pick(3)
            v.wait_ge(s_unp, NG)
            v.tensor_tensor(tokens(NG - 1), tokens(NG - 1), unpicked[NG - 1], ALU.subtract).then_inc(s_pick[NG - 1], 1)
            v.wait_ge(s_pool, NG)
            v.wait_ge(s_rsum, NG)
            v.tensor_tensor(pooled[:, :, :], psum[2][:, 0:NG * C].rearrange("p (g c) -> p g c", c=C),
                            rsum[:, :].unsqueeze(2).to_broadcast([128, NG, C]), ALU.mult).then_inc(s_pe, 1)
            v.wait_ge(s_mask, QUAD * QUAD)
            v.tensor_tensor(rmask[:, :, :], rsum[:, :].unsqueeze(2).to_broadcast([128, NG, QUAD]),
                            mask[:, :].unsqueeze(1).to_broadcast([128, NG, QUAD]), ALU.mult).then_inc(s_rsum, 1)
            v.wait_ge(s_pe, 1)
            v.tensor_reduce(pmean[:, :], pooled[:, :, :], AX.X, ALU.add).then_inc(s_pe, 1)
            v.wait_ge(s_pe, 2)
            v.scalar_tensor_tensor(pooled[:, :, :], pmean[:, :].unsqueeze(2).to_broadcast([128, NG, C]), -1.0 / C,
                                   pooled[:, :, :], ALU.mult, ALU.add).then_inc(s_pe, 1)
            for k in range(4):
                v.wait_ge(s_ht, k + 1)
                v.tensor_copy(hid_t[:, 2 * k:2 * k + 2, :, :].rearrange("p q k j -> p (q k j)"), HT_BANKS[k][:, :]) \
                    .then_inc(s_hte, 1)
            for m in range(2):
                v.wait_ge(s_o, m + 1)
                v.tensor_tensor(o_t[:, :, B * m:B * m + B].rearrange("p i (q j) -> p i q j", j=QUAD),
                                OT_BANKS[m][0:C, :].rearrange("p (q j i) -> p i q j", q=4, j=QUAD)[:, 0:B, :, :],
                                b2[:, B * m:B * m + B].rearrange("p (q j) -> p q j", j=QUAD).unsqueeze(1)
                                .to_broadcast([C, B, 4, QUAD]), ALU.add).then_inc(s_oe, 1)
            v.wait_ge(s_ot, 1)
            v.wait_ge(s_rsum, NG + 1)
            for g in range(NG):
                v.tensor_tensor(o_blk[:, g, :, :], OB_BANK[:, C * g:C * g + C].unsqueeze(1).to_broadcast([128, QUAD, C]),
                                rmask[:, g, :].unsqueeze(2).to_broadcast([128, QUAD, C]), ALU.mult).then_inc(s_ob, 1)
            for n in range(2 * NB):
                b, k = n // 2, n % 2
                v.wait_ge(s_y, n + 1)
                if b >= YS and k == 0:
                    v.wait_ge(s_out[b % YS], 2 * DMA * (b // YS))
                v.tensor_tensor(y[:, b % YS, 512 * k:512 * k + 512], Y_BANKS[n % 8][:, :],
                                xc[:, b, 4 * k:4 * k + 4, :].rearrange("p t k -> p (t k)"), ALU.add).then_inc(s_ye, 1)

        @block.tensor
        def _(pe):
            def turn(out_, in_, rows):
                return pe.transpose(out_, in_, ident[0:rows, 0:rows])

            def conv_rows(t, i):
                n, par = RT * t.n + i, i % 2
                if i == 0:
                    pe.wait_ge(s_stk, DMA * NSTK * (t.n + 1))
                    for h in range(2):
                        pe.wait_ge(s_xlo[h], t.n + 1)
                if not (known(t.n) and n < 2):
                    pe.wait_ge(s_ig, 2 * (n - 1))
                for gate in range(4):
                    bank = (ps_of, ps_ig)[gate // 2][par]
                    cols = slice(COLS * (gate % 2), COLS * (gate % 2) + COLS)
                    gate_w = slice(C * GATE_ORDER[gate], C * GATE_ORDER[gate] + C)
                    above = x_parts[1 - t.par if i == 0 else t.par]
                    for m, (w, stack, row) in enumerate(((w_hi[:, X_PARTS[0], gate_w], above, (i - 1) % RT),
                                                         (w_hi[:, X_PARTS[1], gate_w], x_parts[t.par], i),
                                                         (w_lo[:, X_PAIR, gate_w], x_pair[t.par], i))):
                        for h in range(2):
                            ins = pe.matmul(bank[half(h), cols], w, stack[h][:, row, :],
                                            start=gate % 2 == 0 and m == 0, stop=False)
                ins.then_inc(s_conv, 1)

            def conv_state(t, i, between=None):
                n, par = RT * t.n + i, i % 2
                pe.wait_ge(s_hlo, 2 * n + 2)
                for pair in range(2):
                    bank = (ps_of, ps_ig)[pair][par]
                    for m, (w, stack, tap) in enumerate([(w_hi, h_stk, 0), (w_hi, h_stk, 1), (w_hi, h_stk, 2),
                                                         (w_lo, h_stk, 2), (w_lo, h_pair, 0)]):
                        n_stack = H_PAIR if m == 4 else H_PARTS[tap]
                        if m == 4 and pair == 0:
                            pe.wait_ge(s_hpair, 4 * n + 4)
                        for gate in (2 * pair, 2 * pair + 1):
                            cols = slice(COLS * (gate % 2), COLS * (gate % 2) + COLS)
                            for h in range(2):
                                ins = pe.matmul(bank[half(h), cols], w[:, n_stack, C * GATE_ORDER[gate]:][:, 0:C],
                                                stack[par][h][:, :, tap:tap + W], start=False,
                                                stop=m == 4 and gate % 2 == 1)
                    ins.then_inc((s_gof, s_gig)[pair], 1)
                    if pair == 0 and between:
                        turn_x1(between)

            def turn_in(banks, image):
                for k in range(2):
                    for b in range(4):
                        ins = turn(banks[k][:, 128 * b:128 * b + 128], image(4 * k + b), 128)
                    ins.then_inc(s_p0t, 1)

            def turn_r0(t):
                pe.wait_ge(s_r0, t.n + 1)
                turn(ps_r[0:B, 0:TOK], r0[:, t.par, :], 128).then_inc(s_r0t, 1)

            def turn_x1(t):
                pe.wait_ge(s_x1, RT * (t.n + 1))
                for k in range(2):
                    for b in range(4):
                        ins = turn(ps_t[k][:, 128 * b:128 * b + 128], x1t[:, t.par, 4 * k + b, :], 128)
                    ins.then_inc(s_ft, 1)

            def logits(t):
                for g in range(NG):
                    for j in range(2):
                        ins = pe.matmul(ps_lg[C * j:C * j + C, TOK * g:TOK * g + TOK], gw[:, :],
                                        x1t[:, t.par, 2 * g + j, :], start=g == 0, stop=g == NG - 1)
                ins.then_inc(s_lg, 1)

            def turn_r1(t):
                pe.wait_ge(s_r1, t.n + 1)
                turn(ps_r[0:B, 0:TOK], r1[:, :], 128).then_inc(s_r1t, 1)

            def phase(t, first=False, left=AHEAD):
                for i in range(RT):
                    conv_state(t, i, between=None if first or i else t.shift(-1))
                    if i == 1 and left >= AHEAD:
                        if first:
                            pe.wait_ge(s_bn0, 2 * AHEAD)
                            turn_in(ps_t, lambda b: xc[:, b, AHEAD, :])
                        else:
                            pe.wait_ge(s_xtok, 2 * t.n)
                            pe.wait_ge(s_xin, 2 * DMA * t.n)
                            turn_in(ps_t, lambda b: x_in[:, b, :])
                    if i == 1 and not first:
                        logits(t.shift(-1))
                    if i < RT - 1:
                        conv_rows(t, i + 1)
                    elif left > 0:
                        conv_rows(t.shift(1), 0)
                    if i == 0 and left > 1:
                        turn_r0(t.shift(2))
                    if i == 2 and not first:
                        if left > 1:
                            pe.wait_ge(s_r0c, t.n + 2)
                        turn_r1(t.shift(-1))

            t0, t7 = Tile(0, 0, 0), Tile(NT - 1, (NT - 1) // 2, 1)
            pe.wait_ge(s_const, 2)
            pe.wait_ge(s_x[0], 2 * DMA)
            turn_in(ps_t, lambda b: xc[:, b, 0, :])
            pe.wait_ge(s_x[1], 2 * DMA)
            turn_in(psum[6:8], lambda b: xc[:, b, 1, :])
            for k in range(2):
                pe.wait_ge(s_xs, k + 1)
                for b in range(4):
                    ins = turn(ps_t[k][:, 128 * b:128 * b + 128],
                               xtok[:, 0, 8 * k + 2 * b:8 * k + 2 * b + 2, :].rearrange("p b c -> p (b c)"), 128)
                ins.then_inc(s_xst, 1)
            for n in range(len(W_STACKS)):
                pe.wait_ge(s_wstep, 3 + 4 * (n + 1))
                for m in range(2):
                    ins = turn(psum[n // 2][:, GATES * (n % 2) + 128 * m:][:, 0:128], w_stack[:, m, n, :], 128)
                ins.then_inc(s_wt, 1)
            turn_r0(t0.shift(1))
            pe.wait_ge(s_gws, 5)
            turn(ps_lg[:, 256:256 + 2 * E], gw_rows[:, :], 2 * E)
            turn(ps_lg[0:C, 384:384 + E], b2_rows[:, :], E)
            turn(ps_lg[:, 448:452], b_rows[:, 0, :], 4).then_inc(s_gwt, 1)
            pe.wait_ge(s_xlo[1], 1)
            pe.wait_ge(s_x[2], 2 * DMA)
            turn_in(ps_t, lambda b: xc[:, b, 2, :])
            pe.wait_ge(s_const, 15)
            pe.wait_ge(s_wlo, len(W_STACKS))
            conv_rows(t0, 0)
            pe.wait_ge(s_gwc, 2)
            phase(t0, first=True)
            with pe.Fori(0, (NT - 4) // 2) as k:
                t = Tile(2 * k + 1, k, 1)
                phase(t)
                phase(t.shift(1))
            for left in (2, 1, 0):
                phase(t7.shift(-left), left=left)
            turn_x1(t7)
            logits(t7)
            pe.wait_ge(s_r1, NT)
            for g in range(NG):
                for q in range(QUAD):
                    ins = pe.matmul(psum[0][E * q:E * q + E, TOK * g:TOK * g + TOK],
                                    r1[:, QUAD * g + q:QUAD * g + q + 1].to_broadcast([128, E]), ident[:, :],
                                    start=g == 0, stop=g == NG - 1)
            ins.then_inc(s_rb1, 1)

            def turn_picks(g):
                pe.wait_ge(s_pick[g], 1)
                wait(pe, s_ptm, 2 * (g - 1))
                for k in range(2):
                    for m in range(4):
                        ins = turn(PICK_BANKS[2 * (g % 2) + k][:, 128 * m:128 * m + 128], lg[:, g, 4 * k + m, :], 128)
                    ins.then_inc(s_pt, 1)

            def pool(g):
                pe.wait_ge(s_ptm, 2 * g + 2)
                pe.wait_ge(s_xts, NT)
                for m in range(NT):
                    for k in range(QUAD):
                        ins = pe.matmul(psum[2][E * k:E * k + E, C * g:C * g + C], pick_t[:, g % 2, m, E * k:E * k + E],
                                        xtok[:, m, QUAD * g + k, :], start=g + m == 0,
                                        stop=g == NG - 1 and m == NT - 1)
                ins.then_inc(s_pool, 1)

            turn_picks(0)
            for g in range(NG):
                if g + 1 < NG:
                    turn_picks(g + 1)
                pool(g)
            pe.wait_ge(s_pe, 3)
            for g in range(NG):
                ins = turn(psum[3][0:C, 128 * g:128 * g + 128], pooled[:, g, :], 128)
            ins.then_inc(s_po, 1)
            pe.wait_ge(s_w12, 3 * DMA)
            pe.wait_ge(s_pot, 1)
            for k in range(4):
                for m in range(2):
                    for j in range(QUAD):
                        e = QUAD * (2 * k + m) + j
                        ins = pe.matmul(HID_BANKS[k][E * j:E * j + E, H * m:H * m + H], pool_t[:, e, :], w1s[:, e, :],
                                        start=m == 0, stop=m == 1)
                ins.then_inc(s_hid, 1)
            for k in range(4):
                pe.wait_ge(s_gelu, k + 1)
                for m in range(4):
                    ins = turn(HT_BANKS[k][:, 128 * m:128 * m + 128],
                               hid[:, 2 * k + m // 2, 128 * (m % 2):128 * (m % 2) + 128], 128)
                ins.then_inc(s_ht, 1)
            for q in range(E // QUAD):
                if q % 2 == 0:
                    pe.wait_ge(s_hte, q // 2 + 1)
                for k in range(2):
                    for j in range(QUAD):
                        ins = pe.matmul(psum[0][E * j:E * j + E, C * q:C * q + C], hid_t[:, q, k, E * j:E * j + E],
                                        w2s[:, k, QUAD * q + j, :], start=q + k == 0,
                                        stop=q == E // QUAD - 1 and k == 1)
            ins.then_inc(s_oi, 1)
            pe.wait_ge(s_oie, 1)
            for m in range(2):
                for q in range(4):
                    ins = turn(OT_BANKS[m][0:C, 128 * q:128 * q + 128], o_img[:, C * (4 * m + q):][:, 0:C], 128)
                ins.then_inc(s_o, 1)
            pe.wait_ge(s_oe, 2)
            for g in range(NG):
                ins = turn(OB_BANK[:, C * g:C * g + C],
                           o_t[:, QUAD * g:QUAD * g + QUAD, :].rearrange("p i e -> p (i e)"), C)
            ins.then_inc(s_ot, 1)
            for n in range(2 * NB):
                b, k = n // 2, n % 2
                g, j = b // 2, b % 2
                if n % 4 == 0:
                    pe.wait_ge(s_ob, 1 if n == 0 else NG)
                if n >= 8 and k == 0:
                    pe.wait_ge(s_ye, n - 6)
                pe.matmul(Y_BANKS[n % 8][:, :], o_blk[:, g, 2 * j:2 * j + 2, :].rearrange("p h c -> p (h c)"),
                          lg[:, g, 4 * k:4 * k + 4, :].rearrange("p t k -> p (t k)"),
                          start=True, stop=True).then_inc(s_y, 1)


_INS = ["x", "L0_conv_w_itos", "L0_conv_b_itos", "L0_conv_w_stos", "L0_conv_b_stos", "L0_conv_h0", "L0_conv_c0",
        "L0_ffn_gate_w", "L0_ffn_gate_b", "L0_ffn_weight1", "L0_ffn_weight2"]


def kernel(**inputs):
    import numpy as np
    import concourse.bacc as bacc
    from concourse.bass_utils import run_bass_kernel_spmd

    nc = bacc.Bacc("TRN2", target_bir_lowering=False, num_devices=1)
    arrays, args = {}, []
    for name in _INS:
        a = np.ascontiguousarray(inputs[name])
        arrays[f"in_{name}"] = a
        args.append(nc.dram_tensor(f"in_{name}", a.shape, F32, kind="ExternalInput").ap())
    args.append(nc.dram_tensor("out", (B, C, S, W), F32, kind="ExternalOutput").ap())
    args.append(nc.dram_tensor("scratch0", (2, B, TOK), F32, kind="Internal").ap())
    args.append(nc.dram_tensor("scratch1", (B, TOK), F32, kind="Internal").ap())
    metaformer(nc, *args)
    got = run_bass_kernel_spmd(nc, [arrays], core_ids=[0])
    return got.results[0]["out"]
```

```python
from contextlib import ExitStack

import concourse.bass as bass
from concourse import mybir

F32 = mybir.dt.float32
F16 = mybir.dt.float16
ACT = mybir.ActivationFunctionType
ALU = mybir.AluOpType
AX = mybir.AxisListType

B, C, S, W = 16, 64, 32, 32
E, K, H = 32, 8, 256
NB = B // 2
HALF_E = E // 2
COLS = NB * W
RT = 4
TOK = RT * W
NT = S // RT
NG = NB // 2
QUAD = 4
GATES = 4 * C
GATE_ORDER = (3, 2, 0, 1)
PAD = W + 2
W_STACKS = ((1, 0, 0), (1, 1, 1), (1, 2, 2), (1, 0, 1), (0, 0, 0), (0, 1, 1), (0, 0, 1))
H_PARTS, H_PAIR, X_PARTS, X_PAIR = (0, 1, 2), 3, (4, 5), 6
H_STACKS, X_STACKS = range(4), range(4, 7)
EPS_CONV, EPS_FFN = 1e-6, 1e-5
EARLY = 6
YS = 4
DMA = 16
BN = 6
X_LOADS = ((0, 1), (1, 2), (2, 4), (4, 8))
AHEAD = 3


class Tile:

    def __init__(self, n, half, par):
        self.n, self.half, self.par = n, half, par

    def shift(self, d):
        p = self.par + d
        return Tile(self.n + d, self.half + p // 2, p % 2)


def known(v):
    return isinstance(v, int)


def wait(eng, sem, value):
    if not known(value) or value > 0:
        eng.wait_ge(sem, value)


def metaformer(nc, x, w_itos, b_itos, w_stos, b_stos, h0, c0, gate_w, gate_b, w1, w2, out, scratch0, scratch1):
    ctx = ExitStack()
    with ctx:
        def sb(name, shape, dt=F32):
            return ctx.enter_context(nc.sbuf_tensor(name, shape, dt))

        def sem(name):
            return ctx.enter_context(nc.semaphore(name))

        ident = sb("ident", [128, 128])
        w_rows = sb("w_rows", [128, 2, 2, 3 * C])
        w_mean = sb("w_mean", [128, 2, 2])
        w_stack = sb("w_stack", [128, 2, len(W_STACKS), 128])
        w_hi = sb("w_hi", [128, len(W_STACKS), GATES], F16)
        w_lo = sb("w_lo", [128, len(W_STACKS), GATES], F16)
        b_rows = sb("b_rows", [4, 2, 2 * C])
        bias = sb("bias", [128, 4])
        gw_rows = sb("gw_rows", [2 * E, 2 * C])
        gw_mean = sb("gw_mean", [2 * E, 1])
        gw = sb("gw", [128, 2 * E])
        gbias = sb("gbias", [128, 1])
        pow_exp = sb("pow_exp", [128, B])
        w1s = sb("w1s", [C + 1, E, H])
        w2s = sb("w2s", [128, 2, E, C])
        b2_rows = sb("b2_rows", [E, C])
        b2 = sb("b2", [C, E])
        xc = sb("xc", [128, NB, NT, TOK])
        x_in = sb("x_in", [128, NB, TOK])
        st0 = sb("st0", [128, 2, B, BN])
        v0 = sb("v0", [128, 2, 4, B])
        r0 = sb("r0", [128, 2, B])
        r0t = sb("r0t", [B, 2, TOK])
        rb_xr = sb("rb_xr", [128, 2, NB * TOK])
        rb = rb_xr[:, 0, :].rearrange("p (b t) -> p b t", b=NB)
        xr = rb_xr[:, 1, :].rearrange("p (s b w) -> p s b w", s=RT, b=NB)
        x_stks = sb("x_stks", [128, 2, 2, 2, RT * COLS], F16)
        x_parts = [[x_stks[:, p, h, 0, :].rearrange("p (s c) -> p s c", s=RT) for h in range(2)] for p in range(2)]
        x_pair = [[x_stks[:, p, h, 1, :].rearrange("p (s c) -> p s c", s=RT) for h in range(2)] for p in range(2)]
        h_stk = [[sb(f"h_stk{p}{h}", [128, NB, PAD], F16) for h in range(2)] for p in range(2)]
        h_pair = [[sb(f"h_pair{p}{h}", [128, NB, PAD], F16) for h in range(2)] for p in range(2)]
        sg_o = sb("sg_o", [128, COLS])
        sg_f = sb("sg_f", [128, COLS])
        sg_i = sb("sg_i", [128, COLS])
        th_g = sb("th_g", [128, COLS])
        h32 = sb("h32", [128, 2, COLS])
        cell = sb("cell", [128, 2, COLS])
        fc = sb("fc", [128, COLS])
        ig = sb("ig", [128, COLS])
        x1t = sb("x1t", [128, 2, NB, TOK])
        xtok = sb("xtok", [128, NT, B, C])
        st1 = sb("st1", [128, B, BN])
        v1 = sb("v1", [128, 4, B])
        r1 = sb("r1", [128, B])
        r1t = sb("r1t", [B, TOK])
        rbf = sb("rbf", [128, NG, TOK])
        lgr = sb("lgr", [128, NG, TOK])
        lg = sb("lg", [128, NG, NT, TOK])
        cands = sb("cands", [128, NG, 2 * K])
        top = sb("top", [128, NG, K])
        top_e = sb("top_e", [128, NG, K])
        gb_max = sb("gb_max", [128, NG])
        gb_sub = sb("gb_sub", [128, NG])
        esum = sb("esum", [128, NG])
        rsum = sb("rsum", [128, NG])
        pooled = sg_o[:, :].rearrange("p (g c) -> p g c", c=C)
        pmean = sb("pmean", [128, NG])
        mask = sb("mask", [128, QUAD])
        rmask = sb("rmask", [128, NG, QUAD])
        tail_room = x_stks[:, :, :, :, :].rearrange("p a b c k -> p (a b c k)").bitcast(F32)
        unpicked = [tail_room[:, NT * TOK * g:NT * TOK * g + NT * TOK] for g in range(NG)]
        y = tail_room.rearrange("p (a k) -> p a k", a=YS)
        hid = xtok[:, 0:2, :, :].rearrange("p a b c -> p (a b c)").rearrange("p (q h) -> p q h", h=H)
        hid_t = rb_xr[:, :, :].rearrange("p a (q k j) -> p (a q) k j", k=2, j=128)
        pool_t = w_stack[0:C + 1, :, :, :].rearrange("p a n k -> p (a n k)")[:, 0:2 * B * E] \
            .rearrange("p (e i) -> p e i", e=E)
        lgr_last = h32[:, :, :].rearrange("p a (g t) -> p (a g) t", t=TOK)
        o_img = h32[:, :, :].rearrange("p a k -> p (a k)")
        o_t = lgr[0:C, :, :].rearrange("p g (i e) -> p (g i) e", e=E)
        o_blk = x1t[:, 0, :, :].rearrange("p b k -> p (b k)").rearrange("p (g q c) -> p g q c", g=NG, q=QUAD)
        pick_t = x1t[:, :, :, :]

        psum = [ctx.enter_context(nc.psum_tensor(f"ps{i}", [128, 512], F32)) for i in range(8)]
        ps_of, ps_ig = psum[0:2], psum[2:4]
        ps_t = psum[4:6]
        ps_lg, ps_r = psum[6], psum[7]
        PICK_BANKS = psum[4:6] + psum[0:2]
        RB_BANKS = psum[0], psum[1], psum[3], psum[7]
        POOL_BANKS = psum[2], psum[6], psum[3], psum[7]
        PT_BANK = psum[4]
        HID_BANKS = psum[0:2] + psum[4:6]
        HT_BANKS = psum[2:4] + psum[6:8]
        O_BANKS, OT_BANKS, OB_BANK = psum[0:2], psum[4:6], psum[0]
        Y_BANKS = psum[6:8] + psum[2:4] + [psum[1]] + psum[4:6] + [psum[0]]

        s_const = sem("s_const")
        s_pool_room = sem("s_pool_room")
        s_conv_w_in = sem("s_conv_w_in")
        s_gate_w_in = sem("s_gate_w_in")
        s_mask = sem("s_mask")
        s_bias_kept = sem("s_bias_kept")
        s_gate_centered = sem("s_gate_centered")
        s_gate_turned = sem("s_gate_turned")
        s_gate_kept = sem("s_gate_kept")
        s_raw_logits = sem("s_raw_logits")
        s_rsum = sem("s_rsum")
        s_x_weights = sem("s_x_weights")
        s_w_turned = sem("s_w_turned")
        s_w_hi = sem("s_w_hi")
        s_w_lo = sem("s_w_lo")
        s_h_weights = sem("s_h_weights")
        s_bias_in = sem("s_bias_in")
        s_bias_sum = sem("s_bias_sum")
        s_bias_turned = sem("s_bias_turned")
        s_table = sem("s_table")
        s_row_below = sem("s_row_below")
        s_expert_w_in = sem("s_expert_w_in")
        s_gate_zeroed = sem("s_gate_zeroed")
        s_init_in = sem("s_init_in")
        s_x = [sem(f"s_xload{n}") for n in range(len(X_LOADS))]
        s_h_pair = sem("s_h_pair")
        s_x_turned = sem("s_x_turned")
        s_x_stats = sem("s_x_stats")
        s_x_var = sem("s_x_var")
        s_r0 = sem("s_r0")
        s_r0_turned = sem("s_r0_turned")
        s_r0_kept = sem("s_r0_kept")
        s_r0_stored = sem("s_r0_stored")
        s_rb_in = sem("s_rb_in")
        s_xr = sem("s_xr")
        s_x_hi = [sem(f"s_x_hi{h}") for h in range(2)]
        s_x_lo = [sem(f"s_x_lo{h}") for h in range(2)]
        s_x_again = sem("s_x_again")
        s_x0_scaled = sem("s_x0_scaled")
        s_x0_turned = sem("s_x0_turned")
        s_stacked = sem("s_stacked")
        s_conv = sem("s_conv")
        s_gates_of = sem("s_gates_of")
        s_gates_ig = sem("s_gates_ig")
        s_sg_o = sem("s_sg_o")
        s_sg_f = sem("s_sg_f")
        s_act_ig = sem("s_act_ig")
        s_h32 = sem("s_h32")
        s_h_hi = sem("s_h_hi")
        s_h_lo = sem("s_h_lo")
        s_cell = sem("s_cell")
        s_prod = sem("s_prod")
        s_x1 = sem("s_x1")
        s_x1_kept = sem("s_x1_kept")
        s_x1_turned = sem("s_x1_turned")
        s_xtok = sem("s_xtok")
        s_x1_stats = sem("s_x1_stats")
        s_x1_var = sem("s_x1_var")
        s_r1 = sem("s_r1")
        s_xtok_scaled = sem("s_xtok_scaled")
        s_r1_spread = sem("s_r1_spread")
        s_r1_turned = sem("s_r1_turned")
        s_r1_kept = sem("s_r1_kept")
        s_r1_stored = sem("s_r1_stored")
        s_rbf_in = sem("s_rbf_in")
        s_logits = sem("s_logits")
        s_scaled_logits = sem("s_scaled_logits")
        s_last_logits = sem("s_last_logits")
        s_early = sem("s_early")
        s_top = sem("s_top")
        s_sub = sem("s_sub")
        s_exp = sem("s_exp")
        s_unpicked = sem("s_unpicked")
        s_pick = [sem(f"s_pick{g}") for g in range(NG)]
        s_picks_turned = sem("s_picks_turned")
        s_picks_kept = sem("s_picks_kept")
        s_pooled = sem("s_pooled")
        s_centered = sem("s_centered")
        s_pooled_turned = sem("s_pooled_turned")
        s_pool_t = sem("s_pool_t")
        s_hidden = sem("s_hidden")
        s_gelu = sem("s_gelu")
        s_hid_turned = sem("s_hid_turned")
        s_hid_t = sem("s_hid_t")
        s_o_turned = sem("s_o_turned")
        s_o_t = sem("s_o_t")
        s_o_blocks = sem("s_o_blocks")
        s_o_blk = sem("s_o_blk")
        s_y = sem("s_y")
        s_y_sum = sem("s_y_sum")
        s_o_img = sem("s_o_img")
        s_o_img_kept = sem("s_o_img_kept")
        s_out = [sem(f"s_out{p}") for p in range(YS)]

        x_cm = x.rearrange("(a b) c s w -> a c b (s w)", a=2)
        out_cm = out.rearrange("(a b) c s w -> a c b (s w)", a=2)

        NSTK = 4

        def half(h):
            return slice(C * h, C * h + C)

        def hi_rows(h):
            return slice(C * h, C * h + C)

        def lo_rows(h):
            return slice(C * (1 - h), C * (1 - h) + C)

        block = ctx.enter_context(nc.Block())

        @block.sync
        def _(q):
            def load_x_in(t):
                q.wait_ge(s_x_turned, 2 * t.n)
                for h in range(2):
                    q.dma_start(x_in[half(h), :, :], x_cm[h, :, :, bass.ds(t.n * TOK, TOK)]).then_inc(s_x_again, DMA)

            def store_r0(t):
                q.wait_ge(s_r0_kept, t.n)
                q.dma_start(scratch0[t.par], r0t[:, t.par, :]).then_inc(s_r0_stored, DMA)

            def spread_r0(t):
                q.wait_ge(s_r0_stored, DMA * t.n)
                for h in range(2):
                    q.dma_start(rb[half(h), :, :], scratch0[t.par].rearrange("(b h) t -> h b t", h=2)[h]
                                .partition_broadcast(C)).then_inc(s_rb_in, DMA)

            def stack_x(t):
                for h in (1, 0):
                    q.wait_ge(s_x_hi[h], t.n + 1)
                    hi = x_parts[t.par][h][hi_rows(h), :, :]
                    pair = x_pair[t.par][h]
                    q.dma_start(pair[0:C, 1:RT, :], hi[:, 0:RT - 1, :]).then_inc(s_stacked, DMA)
                    q.dma_start(pair[C:2 * C, :, :], hi).then_inc(s_stacked, DMA)
                for h in range(2):
                    q.dma_start(x_pair[1 - t.par][h][0:C, 0:1, :], x_parts[t.par][h][hi_rows(h), RT - 1:RT, :]) \
                        .then_inc(s_row_below, DMA)

            def spread_r1(t):
                q.wait_ge(s_r1_kept, t.n + 1)
                q.dma_start(scratch1[:, :], r1t[:, :]).then_inc(s_r1_stored, DMA)
                q.wait_ge(s_r1_stored, DMA * (t.n + 1))
                r_g = scratch1.rearrange("(g q) t -> q g t", q=QUAD)
                for k in range(QUAD):
                    q.dma_start(rbf[E * k:E * k + E, :, :], r_g[k].partition_broadcast(E)).then_inc(s_rbf_in, DMA)

            def keep_x1(t):
                q.wait_ge(s_x1, RT * (t.n + 1))
                q.dma_start(xc[:, :, bass.ds(t.n, 1), :], x1t[:, t.par, :, :].unsqueeze(2)).then_inc(s_x1_kept, DMA)

            def phase(t, first=False, left=AHEAD):
                if not first and left >= AHEAD:
                    load_x_in(t.shift(AHEAD))
                if not first:
                    keep_x1(t.shift(-1))
                if left > 0:
                    stack_x(t.shift(1))
                if left > 1:
                    store_r0(t.shift(2))
                    spread_r0(t.shift(2))
                if not first:
                    spread_r1(t.shift(-1))

            t0, t7 = Tile(0, 0, 0), Tile(NT - 1, (NT - 1) // 2, 1)
            def load_x(k):
                a, b = X_LOADS[k]
                for h in range(2):
                    q.dma_start(xc[half(h), :, a:b, :], x_cm[h, :, :, a * TOK:b * TOK]
                                .rearrange("c b (n t) -> c b n t", t=TOK)).then_inc(s_x[k], DMA)

            load_x(0)
            for a in range(2):
                for n, w in enumerate((w_itos, w_stos)):
                    q.dma_start(w_rows[:, a, n, :], w[128 * a:128 * a + 128].rearrange("o c k one -> o (c k one)")) \
                        .then_inc(s_conv_w_in, DMA)
            load_x(1)
            for h in range(2):
                q.dma_start(h32[half(h), 1, :].rearrange("p (b w) -> p b w", w=W),
                            h0.rearrange("c w one -> c one w").to_broadcast([C, NB, W])).then_inc(s_init_in, DMA)
                q.dma_start(cell[half(h), 0, :].rearrange("p (b w) -> p b w", w=W),
                            c0.rearrange("c w one -> c one w").to_broadcast([C, NB, W])).then_inc(s_init_in, DMA)
            for h in range(2):
                for n, b in enumerate((b_itos, b_stos)):
                    q.dma_start(b_rows[:, n, half(h)], b.rearrange("(g c) -> g c", c=C)).then_inc(s_bias_in, DMA)
            load_x(2)
            q.wait_ge(s_gate_zeroed, 1)
            for h in range(2):
                q.dma_start(gw_rows[E * h:E * h + E, C * h:C * h + C], gate_w).then_inc(s_gate_w_in, DMA)
            for k in range(QUAD):
                q.dma_start(gbias[E * k:E * k + E, :], gate_b.unsqueeze(1)).then_inc(s_gate_w_in, DMA)
            q.dma_start(b2_rows[:, :], w2[:, H, :]).then_inc(s_gate_w_in, DMA)
            stack_x(t0)
            store_r0(t0.shift(1))
            spread_r0(t0.shift(1))
            load_x(3)
            phase(t0, first=True)
            with q.Fori(0, (NT - 4) // 2) as k:
                t = Tile(2 * k + 1, k, 1)
                phase(t)
                phase(t.shift(1))
            for left in (2, 1, 0):
                phase(t7.shift(-left), left=left)
            keep_x1(t7)
            q.dma_start(w1s[:, :, :], w1.rearrange("e k h -> k e h")).then_inc(s_expert_w_in, DMA)
            for k in range(2):
                q.dma_start(w2s[:, k, :, :], w2[:, 128 * k:128 * k + 128, :].rearrange("e k o -> k e o")) \
                    .then_inc(s_expert_w_in, DMA)
            for b in range(NB):
                q.wait_ge(s_y_sum, 2 * b + 2)
                for h in range(2):
                    q.dma_start(out_cm[h, :, b, :], y[half(h), b % YS, :]).then_inc(s_out[b % YS], DMA)
            for p in range(YS):
                q.wait_ge(s_out[p], 2 * DMA * NB // YS)

        @block.gpsimd
        def _(p):
            p.memset(gw_rows[:, :], 0.0).then_inc(s_gate_zeroed, 1)
            p.memset(ident[:, :], 0.0).then_inc(s_const, 1)
            p.wait_ge(s_const, 1)
            p.affine_select(out=ident[:, :], in_=ident[:, :], compare_op=ALU.not_equal, fill=1.0,
                            base=0, pattern=[[-1, 128]], channel_multiplier=1).then_inc(s_const, 1)
            p.memset(pow_exp[:, :], -0.5).then_inc(s_const, 1)
            for par in range(2):
                for h in range(2):
                    p.memset(h_stk[par][h][:, :, :], 0.0).then_inc(s_const, 1)
                    p.memset(h_pair[par][h][:, :, :], 0.0).then_inc(s_const, 1)
            for h in range(2):
                p.memset(x_parts[1][h][:, RT - 1, :], 0.0).then_inc(s_const, 1)
                p.memset(x_pair[0][h][0:C, 0, :], 0.0).then_inc(s_const, 1)
            p.wait_ge(s_const, 15)

            def rsqrt0(t):
                p.wait_ge(s_x_var, 5 * (t.n + 1))
                if known(t.n) and t.n == 2:
                    p.wait_ge(s_x0_scaled, 2)
                elif not known(t.n) or t.n > 2:
                    p.wait_ge(s_r0_turned, t.n - 2)
                p.tensor_tensor(r0[:, t.par, :], v0[:, t.par, 1, :], pow_exp[:, :], ALU.pow).then_inc(s_r0, 1)

            def rsqrt1(t):
                p.wait_ge(s_x1_var, 5 * (t.n + 1))
                p.tensor_tensor(r1[:, :], v1[:, 1, :], pow_exp[:, :], ALU.pow).then_inc(s_r1, 1)

            def scale_tokens(t):
                p.wait_ge(s_r1, t.n + 1)
                here = xtok[:, bass.ds(t.n, 1), :, :].rearrange("p t b c -> p (t b) c")
                p.tensor_tensor(here, here, r1[:, :].unsqueeze(2).to_broadcast([128, B, C]), ALU.mult) \
                    .then_inc(s_xtok_scaled, 1)

            def residual(t, i):
                n = RT * t.n + i
                p.wait_ge(s_h32, n + 1)
                rows = slice(W * i, W * i + W)
                p.tensor_tensor(x1t[:, t.par, :, rows].unsqueeze(2), xc[:, :, bass.ds(t.n, 1), rows],
                                h32[:, i % 2, :].rearrange("p (b w) -> p b w", w=W).unsqueeze(2), ALU.add) \
                    .then_inc(s_x1, 1)

            def scale_logits(t):
                p.wait_ge(s_raw_logits, t.n + 1)
                p.wait_ge(s_rbf_in, QUAD * DMA * (t.n + 1))
                p.tensor_tensor(lg[:, :, bass.ds(t.n, 1), :], lgr[:, :, :].unsqueeze(2), rbf[:, :, :].unsqueeze(2),
                                ALU.mult).then_inc(s_scaled_logits, 1)

            def scale_rows(t, before):
                p.wait_ge(s_rb_in, 2 * DMA * t.n)
                for h in range(2):
                    p.wait_ge(s_x_lo[h], t.n)
                p.tensor_tensor(xr[:, :, :, :],
                                xc[:, :, 1:, :][:, :, bass.ds(before, 1), :]
                                .rearrange("p b n (s w) -> p (n s) b w", w=W),
                                rb[:, :, :].rearrange("p b (s w) -> p s b w", w=W), ALU.mult).then_inc(s_xr, 1)

            def lo_of_x(t):
                p.wait_ge(s_x_hi[0], t.n + 1)
                p.tensor_tensor(x_parts[t.par][0][lo_rows(0), :, :],
                                xr[half(0), :, :, :].rearrange("p s b w -> p s (b w)"),
                                x_parts[t.par][0][hi_rows(0), :, :], ALU.subtract).then_inc(s_x_lo[0], 1)

            def phase(t, first=False, left=AHEAD):
                if not first:
                    residual(t, 0)
                if left > 0:
                    scale_rows(t.shift(1), t.n)
                if left > 1:
                    rsqrt0(t.shift(2))
                if first:
                    residual(t, 0)
                residual(t, 1)
                if not first:
                    rsqrt1(t.shift(-1))
                if left > 0:
                    if first:
                        p.wait_ge(s_x1, 2)
                    else:
                        p.wait_ge(s_r1, t.n)
                    lo_of_x(t.shift(1))
                    p.wait_ge(s_x_lo[0], t.n + 2)
                residual(t, 2)
                if not first and left > 0:
                    scale_tokens(t.shift(-1))
                residual(t, 3)
                if not first and left > 0:
                    p.wait_ge(s_x1_kept, DMA * t.n)
                    scale_logits(t.shift(-1))

            t0, t7 = Tile(0, 0, 0), Tile(NT - 1, (NT - 1) // 2, 1)
            rsqrt0(t0)
            p.wait_ge(s_bias_in, 4 * DMA)
            p.tensor_tensor(b_rows[:, 0, :], b_rows[:, 0, :], b_rows[:, 1, :], ALU.add).then_inc(s_bias_sum, 1)
            p.wait_ge(s_bias_sum, 1)
            rsqrt0(t0.shift(1))
            p.wait_ge(s_w_turned, len(W_STACKS))
            p.memset(pool_t[:, :, :], 0.0).then_inc(s_pool_room, 1)
            p.wait_ge(s_pool_room, 1)
            p.memset(pool_t[C:C + 1, :, :], 1.0).then_inc(s_pool_room, 1)
            p.wait_ge(s_pool_room, 2)
            phase(t0, first=True)
            p.wait_ge(s_x[-1], 2 * DMA)
            with p.Fori(0, (NT - 4) // 2) as k:
                t = Tile(2 * k + 1, k, 1)
                phase(t)
                phase(t.shift(1))
            for left in (2, 1, 0):
                phase(t7.shift(-left), left=left)
            scale_tokens(t7.shift(-1))
            p.wait_ge(s_xtok_scaled, NT - 1)
            rsqrt1(t7)
            scale_logits(t7.shift(-1))
            p.wait_ge(s_xtok, 2 * NT)
            scale_tokens(t7)
            p.wait_ge(s_unpicked, NG)
            tokens = lg[:, NG - 1, :, :].rearrange("p t k -> p (t k)")
            p.tensor_tensor(tokens, tokens, unpicked[NG - 1], ALU.subtract).then_inc(s_pick[NG - 1], 1)

        @block.scalar
        def _(a):
            def hi_of_x0():
                for h in (1, 0):
                    for k in range(2):
                        a.wait_ge(s_x0_turned, k + 1)
                        ins = a.activation(x_parts[0][h][hi_rows(h), :, 4 * W * k:4 * W * k + 4 * W]
                                           .rearrange("p s (b w) -> p s b w", w=W),
                                           ps_t[k][half(h), :].rearrange("p (b s w) -> p s b w", s=RT, w=W), ACT.Copy)
                    ins.then_inc(s_x_hi[h], 1)

            def hi_of_x(t):
                a.wait_ge(s_conv, RT * t.n - 3)
                for h in (1, 0):
                    a.wait_ge(s_xr, t.n)
                    a.activation(x_parts[t.par][h][hi_rows(h), :, :],
                                 xr[half(h), :, :, :].rearrange("p s b w -> p s (b w)"), ACT.Copy) \
                                     .then_inc(s_x_hi[h], 1)

            def hi_part(n, slot, par):
                for h in range(2):
                    a.activation(h_stk[par][h][hi_rows(h), :, 1:W + 1],
                                 h32[half(h), slot, :].rearrange("p (b w) -> p b w", w=W), ACT.Copy) \
                        .then_inc(s_h_hi, 1)

            def step(t, i, between=None, final=False):
                n, par = RT * t.n + i, i % 2
                a.wait_ge(s_gates_of, n + 1)
                wait(a, s_h32, n)
                a.activation(sg_o[:, :], ps_of[par][:, 0:COLS], ACT.Sigmoid, bias=bias[:, 3:4]).then_inc(s_sg_o, 1)
                if final:
                    return
                wait(a, s_cell, n)
                a.activation(sg_f[:, :], ps_of[par][:, COLS:2 * COLS], ACT.Sigmoid, bias=bias[:, 2:3]) \
                    .then_inc(s_sg_f, 1)
                a.wait_ge(s_h32, n + 1)
                hi_part(n, par, 1 - par)
                if between:
                    keep_tokens(between)
                a.wait_ge(s_gates_ig, n + 1)
                a.activation(sg_i[:, :], ps_ig[par][:, 0:COLS], ACT.Sigmoid, bias=bias[:, 0:1]).then_inc(s_act_ig, 1)
                a.activation(th_g[:, :], ps_ig[par][:, COLS:2 * COLS], ACT.Tanh, bias=bias[:, 1:2]) \
                    .then_inc(s_act_ig, 1)

            def keep_tokens(t):
                for k in range(2):
                    a.wait_ge(s_x1_turned, 2 * t.n + k + 1)
                    a.activation(xtok[:, bass.ds(t.n, 1), 8 * k:8 * k + 8, :].rearrange("p t b c -> p t (b c)"),
                                 ps_t[k][:, :].unsqueeze(1), ACT.Copy).then_inc(s_xtok, 1)

            def keep_r0t(t):
                a.wait_ge(s_r0_turned, t.n)
                if not known(t.n) or t.n > 2:
                    a.wait_ge(s_r0_stored, DMA * (t.n - 2))
                a.activation(r0t[:, t.par, :], ps_r[0:B, 0:TOK], ACT.Copy).then_inc(s_r0_kept, 1)

            def keep_r1t(t):
                a.wait_ge(s_r1_turned, t.n + 1)
                a.activation(r1t[:, :], ps_r[0:B, 0:TOK], ACT.Copy).then_inc(s_r1_kept, 1)

            def keep_logits(t):
                a.wait_ge(s_logits, t.n + 1)
                a.activation(lgr[:, :, :].rearrange("p g t -> p (g t)"), ps_lg[:, :], ACT.Copy) \
                    .then_inc(s_raw_logits, 1)

            def phase(t, first=False, left=AHEAD):
                step(t, 0, between=None if first else t.shift(-1))
                if left > 0:
                    hi_of_x(t.shift(1))
                step(t, 1)
                if left > 1:
                    keep_r0t(t.shift(2))
                step(t, 2)
                if not first and left > 0:
                    keep_r1t(t.shift(-1))
                if not first:
                    keep_logits(t.shift(-1))
                step(t, 3, final=left == 0)
                if left == 0:
                    keep_r1t(t.shift(-1))

            t0, t7 = Tile(0, 0, 0), Tile(NT - 1, (NT - 1) // 2, 1)
            a.wait_ge(s_mask, QUAD * QUAD)
            a.activation(pmean[:, :], mask[:, :], ACT.Sigmoid).then_inc(s_table, 1)
            a.wait_ge(s_conv_w_in, 4 * DMA)
            for n in H_STACKS:
                for d, tap in enumerate(W_STACKS[n][1:]):
                    a.activation(w_stack[:, :, n, C * d:C * d + C], w_rows[:, :, 1, tap:3 * C:3], ACT.Copy) \
                        .then_inc(s_h_weights, 1)

            def hi_of_weights(n):
                a.wait_ge(s_w_turned, min(n // 2 * 2 + 2, len(W_STACKS)))
                a.activation(w_hi[:, n, :], psum[n // 2][:, GATES * (n % 2):GATES * (n % 2) + GATES], ACT.Copy) \
                    .then_inc(s_w_hi, 1)

            for n in H_STACKS:
                hi_of_weights(n)
            a.wait_ge(s_init_in, 4 * DMA)
            a.wait_ge(s_const, 11)
            hi_part(-1, 1, 0)
            hi_of_x0()
            for n in X_STACKS:
                hi_of_weights(n)
            keep_r0t(t0.shift(1))
            a.wait_ge(s_bias_turned, 1)
            a.activation(bias[:, :], ps_lg[:, 448:452], ACT.Copy).then_inc(s_bias_kept, 1)
            a.wait_ge(s_bias_kept, 1)
            phase(t0, first=True)
            with a.Fori(0, (NT - 4) // 2) as k:
                t = Tile(2 * k + 1, k, 1)
                phase(t)
                phase(t.shift(1))
            for left in (2, 1, 0):
                phase(t7.shift(-left), left=left)
            a.wait_ge(s_x1_stats, NT + 1)
            keep_tokens(t7)
            a.wait_ge(s_logits, NT)
            a.activation(lgr_last.rearrange("p g t -> p (g t)"), ps_lg[:, :], ACT.Copy).then_inc(s_raw_logits, 1)

            def exponentials(g):
                a.wait_ge(s_sub, 2 * g + 2)
                tokens = lg[:, g, :, :].rearrange("p t k -> p (t k)")
                a.activation(tokens, tokens, ACT.Exp, bias=gb_sub[:, g:g + 1], accum_out=esum[:, g:g + 1]) \
                    .then_inc(s_exp, 1)
                a.activation(top_e[:, g, :], top[:, g, :], ACT.Exp, bias=gb_sub[:, g:g + 1]).then_inc(s_exp, 1)

            def keep_picks(g):
                if g == 0:
                    a.wait_ge(s_x1_kept, DMA * NT)
                if g > 1:
                    a.wait_ge(s_pooled, g - 1)
                for k in range(2):
                    a.wait_ge(s_picks_turned, 2 * g + k + 1)
                    a.activation(pick_t[:, g % 2, 4 * k:4 * k + 4, :].rearrange("p t e -> p (t e)"),
                                 PICK_BANKS[2 * (g % 2) + k][:, :], ACT.Copy).then_inc(s_picks_kept, 1)

            exponentials(0)
            exponentials(1)
            keep_picks(0)
            exponentials(2)
            keep_picks(1)
            exponentials(3)
            keep_picks(2)
            keep_picks(3)
            a.wait_ge(s_pooled_turned, 1)
            a.wait_ge(s_pool_room, 2)
            for m in range(2):
                experts = slice(HALF_E * m, HALF_E * m + HALF_E)
                a.activation(pool_t[0:C, experts, 0:B],
                             PT_BANK[0:C, :].rearrange("p (i e) -> p e i", e=E)[:, experts, :], ACT.Copy) \
                    .then_inc(s_pool_t, 1)
            for k in range(4):
                a.wait_ge(s_hidden, k + 1)
                a.activation(hid[:, 2 * k:2 * k + 2, :].rearrange("p q h -> p (q h)"), HID_BANKS[k][:, :], ACT.Gelu) \
                    .then_inc(s_gelu, 1)
            for m in range(2):
                a.wait_ge(s_o_img, m + 1)
                a.activation(o_img[:, 4 * C * m:4 * C * m + 4 * C], O_BANKS[m][:, 0:4 * C], ACT.Copy) \
                    .then_inc(s_o_img_kept, 1)

        @block.vector
        def _(v):
            def variances(t, st, var, s_bn, count, s_fin, eps):
                v.wait_ge(s_bn, count)
                v.tensor_tensor(var[:, 0, :], st[:, :, 1], st[:, :, 4], ALU.subtract).then_inc(s_fin, 1)
                v.tensor_scalar(var[:, 1, :], st[:, :, 2], 1.0 / C, eps, ALU.mult, ALU.add).then_inc(s_fin, 1)
                v.wait_ge(s_fin, 5 * t.n + 2)
                v.scalar_tensor_tensor(var[:, 2, :], var[:, 0, :], 0.25, var[:, 0, :], ALU.mult, ALU.mult) \
                    .then_inc(s_fin, 1)
                v.scalar_tensor_tensor(var[:, 3, :], st[:, :, 5], 1.0 / C, var[:, 1, :], ALU.mult, ALU.add) \
                    .then_inc(s_fin, 1)
                v.wait_ge(s_fin, 5 * t.n + 4)
                v.tensor_tensor(var[:, 1, :], var[:, 2, :], var[:, 3, :], ALU.add).then_inc(s_fin, 1)

            def stats0(t, banks, k):
                if k == 0 and (not known(t.n) or t.n > 1):
                    v.wait_ge(s_r0, t.n - 1)
                v.wait_ge(s_x_turned, 2 * t.n + k + 1)
                for b in range(8):
                    ins = v.bn_stats(st0[:, t.par, 8 * k + b, :], banks[k][:, C * b:C * b + C])
                ins.then_inc(s_x_stats, 1)

            def variances0(t):
                variances(t, st0[:, t.par, :, :], v0[:, t.par, :, :], s_x_stats, 2 * t.n + 2, s_x_var, EPS_CONV)

            def scale_tokens0():
                v.wait_ge(s_r0, 1)
                for k in range(2):
                    v.tensor_tensor(xtok[:, 0, 8 * k:8 * k + 8, :], ps_t[k][:, :].rearrange("p (b c) -> p b c", c=C),
                                    r0[:, 0, 8 * k:8 * k + 8].unsqueeze(2).to_broadcast([128, 8, C]), ALU.mult) \
                        .then_inc(s_x0_scaled, 1)

            def lo_of_x0():
                for h in (1, 0):
                    v.wait_ge(s_x_hi[h], 1)
                    for k in range(2):
                        cols = slice(4 * W * k, 4 * W * k + 4 * W)
                        ins = v.tensor_tensor(x_parts[0][h][lo_rows(h), :, cols].rearrange("p s (b w) -> p s b w", w=W),
                                              ps_t[k][half(h), :].rearrange("p (b s w) -> p s b w", s=RT, w=W),
                                              x_parts[0][h][hi_rows(h), :, cols]
                                              .rearrange("p s (b w) -> p s b w", w=W), ALU.subtract)
                    ins.then_inc(s_x_lo[h], 1)

            def lo_of_x(t):
                v.wait_ge(s_x_hi[1], t.n + 1)
                v.tensor_tensor(x_parts[t.par][1][lo_rows(1), :, :],
                                xr[half(1), :, :, :].rearrange("p s b w -> p s (b w)"),
                                x_parts[t.par][1][hi_rows(1), :, :], ALU.subtract).then_inc(s_x_lo[1], 1)

            def lo_part(n, slot, par):
                for h in range(2):
                    v.wait_ge(s_h_hi, 2 * (n + 1) + h + 1)
                    v.tensor_tensor(h_stk[par][h][lo_rows(h), :, 1:W + 1],
                                    h32[half(h), slot, :].rearrange("p (b w) -> p b w", w=W),
                                    h_stk[par][h][hi_rows(h), :, 1:W + 1], ALU.subtract).then_inc(s_h_lo, 1)
                for h in range(2):
                    hi = h_stk[par][h][hi_rows(h), :, 1:W + 1]
                    v.tensor_copy(h_pair[par][h][0:C, :, 1:W + 1], hi).then_inc(s_h_pair, 1)
                    v.tensor_copy(h_pair[par][h][C:2 * C, :, 0:W], hi).then_inc(s_h_pair, 1)

            def step(t, i, final=False):
                n, par = RT * t.n + i, i % 2
                v.wait_ge(s_sg_o, n + 1)
                wait(v, s_cell, n)
                if not (known(t.n) and n < 2):
                    v.wait_ge(s_x1, n - 1)
                v.tensor_tensor(h32[:, par, :], cell[:, par, :], sg_o[:, :], ALU.mult).then_inc(s_h32, 1)
                if final:
                    return
                lo_part(n, par, 1 - par)
                v.wait_ge(s_sg_f, n + 1)
                v.tensor_tensor(fc[:, :], sg_f[:, :], cell[:, par, :], ALU.mult).then_inc(s_prod, 1)
                v.wait_ge(s_act_ig, 2 * n + 2)
                v.tensor_tensor(ig[:, :], sg_i[:, :], th_g[:, :], ALU.mult).then_inc(s_prod, 1)
                v.wait_ge(s_prod, 2 * n + 2)
                v.tensor_tensor(cell[:, 1 - par, :], fc[:, :], ig[:, :], ALU.add).then_inc(s_cell, 1)

            def best_early(g):
                v.wait_ge(s_scaled_logits, EARLY)
                v.max(cands[:, g, 0:K], lg[:, g, 0:EARLY, :].rearrange("p t k -> p (t k)")).then_inc(s_early, 1)

            def stats1(t):
                v.wait_ge(s_xtok, 2 * t.n + 2)
                for b in range(B):
                    ins = v.bn_stats(st1[:, b, :], xtok[:, bass.ds(t.n, 1), b, :].rearrange("p t c -> p (t c)"))
                ins.then_inc(s_x1_stats, 1)

            def variances1(t):
                variances(t, st1, v1, s_x1_stats, t.n + 1, s_x1_var, EPS_FFN)

            def phase(t, first=False, left=AHEAD):
                ahead = t.shift(AHEAD)
                for i in range(RT):
                    step(t, i, final=left == 0 and i == RT - 1)
                    if i == 0 and first:
                        center_gate()
                    if i == 2 and first:
                        keep_gate()
                    if i == 0 and not first:
                        stats1(t.shift(-1))
                    if i == (1 if left >= AHEAD else 0) and not first:
                        variances1(t.shift(-1))
                    if i == 1 and left > 0:
                        lo_of_x(t.shift(1))
                    if i == 2 and left >= AHEAD:
                        stats0(ahead, ps_t, 0)
                    if i == 3 and left >= AHEAD:
                        stats0(ahead, ps_t, 1)
                        variances0(ahead)

            t0, t7 = Tile(0, 0, 0), Tile(NT - 1, (NT - 1) // 2, 1)
            for k in range(QUAD):
                for q in range(QUAD):
                    v.memset(mask[E * k:E * k + E, q:q + 1], float(k == q)).then_inc(s_mask, 1)
            for t, banks in ((t0, ps_t), (t0.shift(1), psum[6:8])):
                stats0(t, banks, 0)
                stats0(t, banks, 1)
                variances0(t)
            scale_tokens0()
            v.wait_ge(s_conv_w_in, 4 * DMA)
            for m in range(2):
                v.tensor_reduce(w_mean[:, m, :], w_rows[:, m, 0, :].rearrange("p (c k) -> p k c", k=3)[:, 0:2, :],
                                AX.X, ALU.add).then_inc(s_x_weights, 1)
            v.wait_ge(s_x_weights, 2)
            v.tensor_scalar(w_mean[:, :, :], w_mean[:, :, :], 1.0 / C, None, ALU.mult).then_inc(s_x_weights, 1)
            v.wait_ge(s_x_weights, 3)
            for n in X_STACKS:
                for d, tap in enumerate(W_STACKS[n][1:]):
                    v.tensor_tensor(w_stack[:, :, n, C * d:C * d + C], w_rows[:, :, 0, tap:3 * C:3],
                                    w_mean[:, :, tap:tap + 1].to_broadcast([128, 2, C]), ALU.subtract) \
                        .then_inc(s_x_weights, 1)
            def lo_of_weights(n):
                v.wait_ge(s_w_hi, min(n // 2 * 2 + 2, len(W_STACKS)))
                v.tensor_tensor(w_lo[:, n, :], psum[n // 2][:, GATES * (n % 2):GATES * (n % 2) + GATES],
                                w_hi[:, n, :], ALU.subtract).then_inc(s_w_lo, 1)

            v.wait_ge(s_init_in, 4 * DMA)
            lo_part(-1, 1, 0)
            lo_of_x0()
            for n in H_STACKS:
                lo_of_weights(n)
            for n in X_STACKS:
                lo_of_weights(n)
            stats0(t0.shift(2), ps_t, 0)
            stats0(t0.shift(2), ps_t, 1)
            variances0(t0.shift(2))

            def center_gate():
                v.wait_ge(s_gate_w_in, (2 + QUAD + 1) * DMA)
                v.tensor_reduce(gw_mean[:, :], gw_rows[:, :], AX.X, ALU.add).then_inc(s_gate_centered, 1)
                v.wait_ge(s_gate_centered, 1)
                v.tensor_scalar(gw_mean[:, :], gw_mean[:, :], 1.0 / C, None, ALU.mult).then_inc(s_gate_centered, 1)
                v.wait_ge(s_gate_centered, 2)
                for h in range(2):
                    blk = gw_rows[E * h:E * h + E, C * h:C * h + C]
                    v.tensor_scalar(blk, blk, gw_mean[E * h:E * h + E, :], None, ALU.subtract) \
                        .then_inc(s_gate_centered, 1)

            def keep_gate():
                v.wait_ge(s_gate_turned, 1)
                v.tensor_copy(gw[:, :], ps_lg[:, 256:256 + 2 * E]).then_inc(s_gate_kept, 1)
                v.tensor_copy(b2[:, :], ps_lg[0:C, 384:384 + E]).then_inc(s_gate_kept, 1)

            phase(t0, first=True)
            with v.Fori(0, (NT - 4) // 2) as k:
                t = Tile(2 * k + 1, k, 1)
                phase(t)
                phase(t.shift(1))
            for left in (2, 1, 0):
                phase(t7.shift(-left), left=left)
            for k in range(2):
                v.wait_ge(s_x1_turned, 2 * NT - 1 + k)
                for b in range(8):
                    ins = v.bn_stats(st1[:, 8 * k + b, :], ps_t[k][:, C * b:C * b + C])
                ins.then_inc(s_x1_stats, 1)
            variances(t7, st1, v1, s_x1_stats, NT + 1, s_x1_var, EPS_FFN)
            for g in range(NG):
                best_early(g)

            def tokens(g):
                return lg[:, g, :, :].rearrange("p t k -> p (t k)")

            def best(g):
                v.wait_ge(s_r1_spread, g + 1)
                v.tensor_tensor(lg[:, g, NT - 1, :], lgr_last[:, g, :], RB_BANKS[g][:, 0:TOK], ALU.mult) \
                    .then_inc(s_last_logits, 1)
                v.wait_ge(s_last_logits, g + 1)
                v.max(cands[:, g, K:2 * K], lg[:, g, EARLY:NT, :].rearrange("p t k -> p (t k)")).then_inc(s_top, 1)
                v.wait_ge(s_top, 2 * g + 1)
                v.max(top[:, g, :], cands[:, g, :]).then_inc(s_top, 1)
                v.wait_ge(s_top, 2 * g + 2)
                v.tensor_tensor(gb_max[:, g:g + 1], top[:, g, 0:1], gbias[:, :], ALU.add).then_inc(s_sub, 1)
                v.wait_ge(s_sub, 2 * g + 1)
                v.tensor_tensor(gb_sub[:, g:g + 1], gbias[:, :], gb_max[:, g:g + 1], ALU.subtract).then_inc(s_sub, 1)

            def pick(g):
                v.wait_ge(s_exp, 2 * g + 2)
                v.match_replace(unpicked[g], top_e[:, g, :], tokens(g), 0.0).then_inc(s_unpicked, 1)
                v.reciprocal(rsum[:, g:g + 1], esum[:, g:g + 1]).then_inc(s_rsum, 1)

            def keep_picked(g):
                v.wait_ge(s_unpicked, g + 1)
                v.tensor_tensor(tokens(g), tokens(g), unpicked[g], ALU.subtract).then_inc(s_pick[g], 1)

            v.wait_ge(s_raw_logits, NT)
            v.wait_ge(s_scaled_logits, NT - 1)
            v.wait_ge(s_early, NG)
            best(0)
            best(1)
            pick(0)
            keep_picked(0)
            pick(1)
            keep_picked(1)
            best(2)
            best(3)
            pick(2)
            keep_picked(2)
            pick(3)
            v.wait_ge(s_rsum, NG)
            v.wait_ge(s_mask, QUAD * QUAD)
            v.tensor_tensor(rmask[:, :, :], rsum[:, :].unsqueeze(2).to_broadcast([128, NG, QUAD]),
                            mask[:, :].unsqueeze(1).to_broadcast([128, NG, QUAD]), ALU.mult).then_inc(s_rsum, 1)
            for g in range(NG):
                v.wait_ge(s_pooled, g + 1)
                v.tensor_scalar(pooled[:, g, :], POOL_BANKS[g][:, 0:C], rsum[:, g:g + 1], None, ALU.mult) \
                    .then_inc(s_centered, 1)
                v.wait_ge(s_centered, 3 * g + 1)
                v.tensor_reduce(pmean[:, g:g + 1], pooled[:, g, :], AX.X, ALU.add).then_inc(s_centered, 1)
                v.wait_ge(s_centered, 3 * g + 2)
                v.scalar_tensor_tensor(pooled[:, g, :], pmean[:, g:g + 1].to_broadcast([128, C]), -1.0 / C,
                                       pooled[:, g, :], ALU.mult, ALU.add).then_inc(s_centered, 1)
            for k in range(4):
                v.wait_ge(s_hid_turned, k + 1)
                v.tensor_copy(hid_t[:, 2 * k:2 * k + 2, :, :].rearrange("p q k j -> p (q k j)"), HT_BANKS[k][:, :]) \
                    .then_inc(s_hid_t, 1)
            for m in range(2):
                v.wait_ge(s_o_turned, m + 1)
                experts = slice(HALF_E * m, HALF_E * m + HALF_E)
                v.tensor_tensor(o_t[:, :, experts].rearrange("p i (q j) -> p i q j", j=QUAD),
                                OT_BANKS[m][0:C, :].rearrange("p (q j i) -> p i q j", q=4, j=QUAD)[:, 0:B, :, :],
                                b2[:, experts].rearrange("p (q j) -> p q j", j=QUAD).unsqueeze(1)
                                .to_broadcast([C, B, 4, QUAD]), ALU.add).then_inc(s_o_t, 1)
            v.wait_ge(s_o_blocks, 1)
            v.wait_ge(s_rsum, NG + 1)
            for g, a, b in ((0, 0, 2), (0, 2, QUAD), (1, 0, QUAD), (2, 0, QUAD), (3, 0, QUAD)):
                v.tensor_tensor(o_blk[:, g, a:b, :], OB_BANK[:, C * g:C * g + C].unsqueeze(1)
                                .to_broadcast([128, b - a, C]),
                                rmask[:, g, a:b].unsqueeze(2).to_broadcast([128, b - a, C]), ALU.mult) \
                    .then_inc(s_o_blk, 1)
            for n in range(2 * NB):
                b, k = n // 2, n % 2
                if b >= YS and k == 0:
                    v.wait_ge(s_out[b % YS], 2 * DMA * (b // YS))
                pieces = 2 if n == 2 * NB - 1 else 1
                for m in range(pieces):
                    v.wait_ge(s_y, n + m + 1)
                    size = 512 // pieces
                    cols = slice(size * m, size * m + size)
                    ins = v.tensor_tensor(y[:, b % YS, 512 * k:512 * k + 512][:, cols], Y_BANKS[(n + m) % 8][:, cols],
                                          xc[:, b, 4 * k:4 * k + 4, :].rearrange("p t k -> p (t k)")[:, cols],
                                          ALU.add)
                ins.then_inc(s_y_sum, 1)

        @block.tensor
        def _(pe):
            def turn(out_, in_, rows):
                return pe.transpose(out_, in_, ident[0:rows, 0:rows])

            def conv_rows(t, i, gates=4):
                n, par = RT * t.n + i, i % 2
                if i == 0:
                    pe.wait_ge(s_stacked, DMA * NSTK * (t.n + 1))
                    if not known(t.n) or t.n > 0:
                        pe.wait_ge(s_row_below, 2 * DMA * t.n)
                    for h in range(2):
                        pe.wait_ge(s_x_lo[h], t.n + 1)
                if not (known(t.n) and n < 2):
                    pe.wait_ge(s_act_ig, 2 * (n - 1))
                for gate in range(gates):
                    bank = (ps_of, ps_ig)[gate // 2][par]
                    cols = slice(COLS * (gate % 2), COLS * (gate % 2) + COLS)
                    gate_w = slice(C * GATE_ORDER[gate], C * GATE_ORDER[gate] + C)
                    above = x_parts[1 - t.par if i == 0 else t.par]
                    for m, (w, stack, row) in enumerate(((w_hi[:, X_PARTS[0], gate_w], above, (i - 1) % RT),
                                                         (w_hi[:, X_PARTS[1], gate_w], x_parts[t.par], i),
                                                         (w_lo[:, X_PAIR, gate_w], x_pair[t.par], i))):
                        for h in range(2):
                            ins = pe.matmul(bank[half(h), cols], w, stack[h][:, row, :],
                                            start=gate % 2 == 0 and m == 0, stop=False)
                ins.then_inc(s_conv, 1)

            def conv_state(t, i, between=None, gates=4):
                n, par = RT * t.n + i, i % 2
                pe.wait_ge(s_h_lo, 2 * n + 2)
                for pair in range((gates + 1) // 2):
                    bank = (ps_of, ps_ig)[pair][par]
                    for m, (w, stack, tap) in enumerate([(w_hi, h_stk, 0), (w_hi, h_stk, 1), (w_hi, h_stk, 2),
                                                         (w_lo, h_stk, 2), (w_lo, h_pair, 0)]):
                        n_stack = H_PAIR if m == 4 else H_PARTS[tap]
                        if m == 4 and pair == 0:
                            pe.wait_ge(s_h_pair, 4 * n + 4)
                        last_gate = min(2 * pair + 1, gates - 1)
                        for gate in range(2 * pair, last_gate + 1):
                            cols = slice(COLS * (gate % 2), COLS * (gate % 2) + COLS)
                            for h in range(2):
                                ins = pe.matmul(bank[half(h), cols], w[:, n_stack, C * GATE_ORDER[gate]:][:, 0:C],
                                                stack[par][h][:, :, tap:tap + W], start=False,
                                                stop=m == 4 and gate == last_gate)
                    ins.then_inc((s_gates_of, s_gates_ig)[pair], 1)
                    if pair == 0 and between:
                        turn_x1(*between)

            def turn_in(banks, image):
                for k in range(2):
                    for b in range(4):
                        ins = turn(banks[k][:, 128 * b:128 * b + 128], image(4 * k + b), 128)
                    ins.then_inc(s_x_turned, 1)

            def turn_r0(t):
                pe.wait_ge(s_r0, t.n + 1)
                turn(ps_r[0:B, 0:TOK], r0[:, t.par, :], 128).then_inc(s_r0_turned, 1)

            def turn_x1(t, stats):
                pe.wait_ge(s_x1, RT * (t.n + 1))
                for k in range(2):
                    if k == 1:
                        pe.wait_ge(s_x_stats, stats)
                    for b in range(4):
                        ins = turn(ps_t[k][:, 128 * b:128 * b + 128], x1t[:, t.par, 4 * k + b, :], 128)
                    ins.then_inc(s_x1_turned, 1)

            def logits(t):
                for g in range(NG):
                    for j in range(2):
                        ins = pe.matmul(ps_lg[C * j:C * j + C, TOK * g:TOK * g + TOK], gw[:, :],
                                        x1t[:, t.par, 2 * g + j, :], start=g == 0, stop=g == NG - 1)
                ins.then_inc(s_logits, 1)

            def turn_r1(t):
                pe.wait_ge(s_r1, t.n + 1)
                turn(ps_r[0:B, 0:TOK], r1[:, :], 128).then_inc(s_r1_turned, 1)

            def phase(t, first=False, left=AHEAD):
                for i in range(RT):
                    conv_state(t, i, between=None if first or i else (t.shift(-1), 2 * NT if left < 2 else 2 * t.n + 6),
                               gates=1 if left == 0 and i == RT - 1 else 4)
                    if i == 2 and left >= AHEAD:
                        if first:
                            pe.wait_ge(s_x_stats, 2 * AHEAD)
                            turn_in(ps_t, lambda b: xc[:, b, AHEAD, :])
                        else:
                            pe.wait_ge(s_xtok, 2 * t.n)
                            pe.wait_ge(s_x_again, 2 * DMA * t.n)
                            turn_in(ps_t, lambda b: x_in[:, b, :])
                    if i == 1 and not first:
                        logits(t.shift(-1))
                    if i < RT - 1:
                        conv_rows(t, i + 1, gates=1 if left == 0 and i == RT - 2 else 4)
                    elif left > 0:
                        conv_rows(t.shift(1), 0)
                    if i == 1 and left > 1:
                        turn_r0(t.shift(2))
                    if i == 1 and first:
                        pe.wait_ge(s_gate_centered, 4)
                        turn(ps_lg[:, 256:256 + 2 * E], gw_rows[:, :], 2 * E)
                        turn(ps_lg[0:C, 384:384 + E], b2_rows[:, :], E).then_inc(s_gate_turned, 1)
                    if i == 3 and first:
                        pe.wait_ge(s_gate_kept, 2)
                    if i == (2 if left > 0 else 3) and not first:
                        if left > 1:
                            pe.wait_ge(s_r0_kept, t.n + 2)
                        turn_r1(t.shift(-1))

            t0, t7 = Tile(0, 0, 0), Tile(NT - 1, (NT - 1) // 2, 1)
            pe.wait_ge(s_const, 2)
            pe.wait_ge(s_x[0], 2 * DMA)
            turn_in(ps_t, lambda b: xc[:, b, 0, :])
            pe.wait_ge(s_x[1], 2 * DMA)
            turn_in(psum[6:8], lambda b: xc[:, b, 1, :])
            def turn_weights(n):
                for m in range(2):
                    ins = turn(psum[n // 2][:, GATES * (n % 2) + 128 * m:][:, 0:128], w_stack[:, m, n, :], 128)
                ins.then_inc(s_w_turned, 1)

            for n in H_STACKS:
                pe.wait_ge(s_h_weights, 2 * n + 2)
                turn_weights(n)
            for k in range(2):
                pe.wait_ge(s_x0_scaled, k + 1)
                for b in range(4):
                    ins = turn(ps_t[k][:, 128 * b:128 * b + 128],
                               xtok[:, 0, 8 * k + 2 * b:8 * k + 2 * b + 2, :].rearrange("p b c -> p (b c)"), 128)
                ins.then_inc(s_x0_turned, 1)
            for n in X_STACKS:
                pe.wait_ge(s_x_weights, 3 + 2 * (n - X_STACKS[0] + 1))
                turn_weights(n)
            turn_r0(t0.shift(1))
            pe.wait_ge(s_bias_sum, 1)
            turn(ps_lg[:, 448:452], b_rows[:, 0, :], 4).then_inc(s_bias_turned, 1)
            pe.wait_ge(s_x_lo[0], 1)
            pe.wait_ge(s_x[2], 2 * DMA)
            turn_in(ps_t, lambda b: xc[:, b, 2, :])
            pe.wait_ge(s_const, 15)
            pe.wait_ge(s_w_lo, len(W_STACKS))
            conv_rows(t0, 0)
            phase(t0, first=True)
            with pe.Fori(0, (NT - 4) // 2) as k:
                t = Tile(2 * k + 1, k, 1)
                phase(t)
                phase(t.shift(1))
            for left in (2, 1, 0):
                phase(t7.shift(-left), left=left)
            turn_x1(t7, 2 * NT)
            logits(t7)
            pe.wait_ge(s_r1_kept, NT - 1)
            pe.wait_ge(s_r1, NT)
            for g in range(NG):
                for q in range(QUAD):
                    ins = pe.matmul(RB_BANKS[g][E * q:E * q + E, 0:TOK],
                                    r1[:, QUAD * g + q:QUAD * g + q + 1].to_broadcast([128, E]), ident[:, :],
                                    start=True, stop=True)
                ins.then_inc(s_r1_spread, 1)

            def turn_picks(g):
                pe.wait_ge(s_pick[g], 1)
                wait(pe, s_picks_kept, 2 * (g - 1))
                for k in range(2):
                    for m in range(4):
                        ins = turn(PICK_BANKS[2 * (g % 2) + k][:, 128 * m:128 * m + 128], lg[:, g, 4 * k + m, :], 128)
                    ins.then_inc(s_picks_turned, 1)

            def pool(g):
                pe.wait_ge(s_picks_kept, 2 * g + 2)
                pe.wait_ge(s_xtok_scaled, NT)
                for m in range(NT):
                    for k in range(QUAD):
                        ins = pe.matmul(POOL_BANKS[g][E * k:E * k + E, 0:C], pick_t[:, g % 2, m, E * k:E * k + E],
                                        xtok[:, m, QUAD * g + k, :], start=m == 0,
                                        stop=m == NT - 1)
                ins.then_inc(s_pooled, 1)

            turn_picks(0)
            for g in range(NG):
                if g + 1 < NG:
                    turn_picks(g + 1)
                pool(g)
            for g in range(NG):
                pe.wait_ge(s_centered, 3 * g + 3)
                ins = turn(PT_BANK[0:C, 128 * g:128 * g + 128], pooled[:, g, :], 128)
            ins.then_inc(s_pooled_turned, 1)
            pe.wait_ge(s_expert_w_in, 3 * DMA)
            for k in range(4):
                if k % 2 == 0:
                    pe.wait_ge(s_pool_t, k // 2 + 1)
                for m in range(2):
                    for j in range(QUAD):
                        e = QUAD * (2 * k + m) + j
                        ins = pe.matmul(HID_BANKS[k][E * j:E * j + E, H * m:H * m + H], pool_t[:, e, :], w1s[:, e, :],
                                        start=m == 0, stop=m == 1)
                ins.then_inc(s_hidden, 1)
            for k in range(4):
                pe.wait_ge(s_gelu, k + 1)
                for m in range(4):
                    ins = turn(HT_BANKS[k][:, 128 * m:128 * m + 128],
                               hid[:, 2 * k + m // 2, 128 * (m % 2):128 * (m % 2) + 128], 128)
                ins.then_inc(s_hid_turned, 1)
            for q in range(E // QUAD):
                if q % 2 == 0:
                    pe.wait_ge(s_hid_t, q // 2 + 1)
                for k in range(2):
                    for j in range(QUAD):
                        ins = pe.matmul(O_BANKS[q // 4][E * j:E * j + E, C * (q % 4):C * (q % 4) + C],
                                        hid_t[:, q, k, E * j:E * j + E], w2s[:, k, QUAD * q + j, :],
                                        start=q % 4 + k == 0, stop=q % 4 == 3 and k == 1)
                if q % 4 == 3:
                    ins.then_inc(s_o_img, 1)
            for m in range(2):
                pe.wait_ge(s_o_img_kept, m + 1)
                for q in range(4):
                    ins = turn(OT_BANKS[m][0:C, 128 * q:128 * q + 128], o_img[:, C * (4 * m + q):][:, 0:C], 128)
                ins.then_inc(s_o_turned, 1)
            pe.wait_ge(s_o_t, 2)
            for g in range(NG):
                ins = turn(OB_BANK[:, C * g:C * g + C],
                           o_t[:, QUAD * g:QUAD * g + QUAD, :].rearrange("p i e -> p (i e)"), C)
            ins.then_inc(s_o_blocks, 1)
            for n in range(2 * NB):
                b, k = n // 2, n % 2
                g, j = b // 2, b % 2
                if n in (0, 2):
                    pe.wait_ge(s_o_blk, 1 if n == 0 else NG + 1)
                if n >= 8 and k == 0:
                    pe.wait_ge(s_y_sum, n - 6)
                pieces = 2 if n == 2 * NB - 1 else 1
                for m in range(pieces):
                    size = 512 // pieces
                    cols = slice(size * m, size * m + size)
                    if m == 1:
                        pe.wait_ge(s_y_sum, n - 6)
                    pe.matmul(Y_BANKS[(n + m) % 8][:, cols], o_blk[:, g, 2 * j:2 * j + 2, :].rearrange("p h c -> p (h c)"),
                              lg[:, g, 4 * k:4 * k + 4, :].rearrange("p t k -> p (t k)")[:, cols],
                              start=True, stop=True).then_inc(s_y, 1)


_INS = ["x", "L0_conv_w_itos", "L0_conv_b_itos", "L0_conv_w_stos", "L0_conv_b_stos", "L0_conv_h0", "L0_conv_c0",
        "L0_ffn_gate_w", "L0_ffn_gate_b", "L0_ffn_weight1", "L0_ffn_weight2"]


def kernel(**inputs):
    import numpy as np
    import concourse.bacc as bacc
    from concourse.bass_utils import run_bass_kernel_spmd

    nc = bacc.Bacc("TRN2", target_bir_lowering=False, num_devices=1)
    arrays, args = {}, []
    for name in _INS:
        a = np.ascontiguousarray(inputs[name])
        arrays[f"in_{name}"] = a
        args.append(nc.dram_tensor(f"in_{name}", a.shape, F32, kind="ExternalInput").ap())
    args.append(nc.dram_tensor("out", (B, C, S, W), F32, kind="ExternalOutput").ap())
    args.append(nc.dram_tensor("scratch0", (2, B, TOK), F32, kind="Internal").ap())
    args.append(nc.dram_tensor("scratch1", (B, TOK), F32, kind="Internal").ap())
    metaformer(nc, *args)
    got = run_bass_kernel_spmd(nc, [arrays], core_ids=[0])
    return got.results[0]["out"]
```
